# Optimizing a Trainium2 kernel written in Bass

```python
import numpy as np
import jax
import jax.numpy as jnp

def _softmax(x, axis=-1):
    return jax.nn.softmax(x, axis=axis)

def _gelu(x):
    return jax.nn.gelu(x, approximate=True)

def _silu(x):
    return jax.nn.silu(x)

def _sigmoid(x):
    return jax.nn.sigmoid(x)

def _layernorm(x, axis=-1, eps=1e-05):
    m = jnp.mean(x, axis=axis, keepdims=True)
    v = jnp.var(x, axis=axis, keepdims=True)
    return (x - m) / jnp.sqrt(v + eps)

def _scatter_add(tgt, idx, src, axis=0):
    return tgt.at[idx].add(src)

def _segment_sum(src, seg, n):
    return jax.ops.segment_sum(src, seg, n)
kernel_name = 'mk_adj_resnorm_d2_adj_r2_f177e2'

def setup_inputs(seed: int=0):
    np.random.seed(seed)
    _w = jnp.asarray

    def _rec_inputs():
        import jax
        import jax.numpy as jnp
        _gk = jax.random.key(seed)
        x = -0.000125 + 0.9999 * jax.random.normal(jax.random.fold_in(_gk, 1), (64, 128, 128), jnp.float32)
        _a = jax.random.bernoulli(jax.random.fold_in(_gk, 2), 0.0625, (128, 128))
        _a = jnp.logical_or(_a, jnp.swapaxes(_a, -1, -2))
        _a = jnp.logical_or(_a, jnp.eye(128, dtype=bool))
        _af = _a.astype(jnp.float32)
        _af = _af * jax.random.uniform(jax.random.fold_in(_gk, 3), (128, 128), jnp.float32, 0.05, 0.000488281)
        adj = _af
        return (x, adj)
    x, adj = _rec_inputs()

    def _L0_gnn_setup():
        import jax, jax.numpy as jnp
        import numpy as np
        B, T, D, H = (64, 1024, 128, 128)
        MAX_SKIP = 4

        def _lstm_last(Wih, Whh, bih, bhh, xs):
            N, _, Hd = xs.shape
            bias = bih + bhh

            def step(carry, x_t):
                h, c = carry
                g = x_t @ Wih.T + h @ Whh.T + bias
                i, f, gg, o = jnp.split(g, 4, axis=-1)
                c = jax.nn.sigmoid(f) * c + jax.nn.sigmoid(i) * jnp.tanh(gg)
                h = jax.nn.sigmoid(o) * jnp.tanh(c)
                return ((h, c), None)
            init = (jnp.zeros((N, Hd), xs.dtype), jnp.zeros((N, Hd), xs.dtype))
            (h_last, _), _ = jax.lax.scan(step, init, jnp.swapaxes(xs, 0, 1))
            return h_last
        key = jax.random.key(seed)
        ks = jax.random.split(key, 8)
        s = 0.05
        x = jax.random.normal(ks[0], (B, T, D), jnp.float32)
        adj = jax.random.uniform(ks[1], (T, T), jnp.float32) / T
        Wg0 = jax.random.normal(ks[2], (D, H), jnp.float32) * s
        bg0 = jnp.zeros((H,), jnp.float32)
        Wg1 = jax.random.normal(ks[3], (H, H), jnp.float32) * s
        bg1 = jnp.zeros((H,), jnp.float32)
        Wih = jax.random.normal(ks[4], (MAX_SKIP, 4 * H, H), jnp.float32) * s
        Whh = jax.random.normal(ks[5], (MAX_SKIP, 4 * H, H), jnp.float32) * s
        bih = jax.random.normal(ks[6], (MAX_SKIP, 4 * H), jnp.float32) * s
        bhh = jax.random.normal(ks[7], (MAX_SKIP, 4 * H), jnp.float32) * s
        return dict(x=x, adj=adj, Wg0=Wg0, bg0=bg0, Wg1=Wg1, bg1=bg1, Wih=Wih, Whh=Whh, bih=bih, bhh=bhh)
    _L0_gnn_all = _L0_gnn_setup()
    _L0_gnn_in = {k: v for k, v in _L0_gnn_all.items() if k in ('Wg0', 'bg0', 'Wg1', 'bg1', 'Wih', 'Whh', 'bih', 'bhh')}
    del _L0_gnn_all

    def _L1_gnn_setup():
        import jax, jax.numpy as jnp
        import numpy as np
        EPS = 1e-05

        def _batchnorm(x, gamma, beta):
            mu = jnp.mean(x, axis=0)
            var = jnp.var(x, axis=0)
            return (x - mu) * jax.lax.rsqrt(var + EPS) * gamma + beta
        key = jax.random.key(seed)
        ks = jax.random.split(key, 4)
        b, n, d, h, o = (32, 1024, 128, 256, 128)
        features = jax.random.normal(ks[0], (b, n, d), dtype=jnp.float32)
        A = jax.random.uniform(ks[1], (n, n), dtype=jnp.float32)
        lim1 = float(np.sqrt(6.0 / (d + h)))
        W1 = jax.random.uniform(ks[2], (h, d), minval=-lim1, maxval=lim1, dtype=jnp.float32)
        b1 = jnp.zeros((h,), jnp.float32)
        lim2 = float(np.sqrt(6.0 / (h + o)))
        W2 = jax.random.uniform(ks[3], (o, h), minval=-lim2, maxval=lim2, dtype=jnp.float32)
        b2 = jnp.zeros((o,), jnp.float32)
        g1 = jnp.ones((h,), jnp.float32)
        be1 = jnp.zeros((h,), jnp.float32)
        g2 = jnp.ones((o,), jnp.float32)
        be2 = jnp.zeros((o,), jnp.float32)
        return {'features': features, 'A': A, 'W1': W1, 'b1': b1, 'g1': g1, 'be1': be1, 'W2': W2, 'b2': b2, 'g2': g2, 'be2': be2}
    _L1_gnn_all = _L1_gnn_setup()
    _L1_gnn_in = {k: v for k, v in _L1_gnn_all.items() if k in ('W1', 'b1', 'g1', 'be1', 'W2', 'b2', 'g2', 'be2')}
    del _L1_gnn_all
    return {'x': x, 'adj': adj, 'L0_gnn_Wg0': _L0_gnn_in['Wg0'], 'L0_gnn_bg0': _L0_gnn_in['bg0'], 'L0_gnn_Wg1': _L0_gnn_in['Wg1'], 'L0_gnn_bg1': _L0_gnn_in['bg1'], 'L0_gnn_Wih': _L0_gnn_in['Wih'], 'L0_gnn_Whh': _L0_gnn_in['Whh'], 'L0_gnn_bih': _L0_gnn_in['bih'], 'L0_gnn_bhh': _L0_gnn_in['bhh'], 'L1_gnn_W1': _L1_gnn_in['W1'], 'L1_gnn_b1': _L1_gnn_in['b1'], 'L1_gnn_g1': _L1_gnn_in['g1'], 'L1_gnn_be1': _L1_gnn_in['be1'], 'L1_gnn_W2': _L1_gnn_in['W2'], 'L1_gnn_b2': _L1_gnn_in['b2'], 'L1_gnn_g2': _L1_gnn_in['g2'], 'L1_gnn_be2': _L1_gnn_in['be2']}

def reference(x, adj, L0_gnn_Wg0, L0_gnn_bg0, L0_gnn_Wg1, L0_gnn_bg1, L0_gnn_Wih, L0_gnn_Whh, L0_gnn_bih, L0_gnn_bhh, L1_gnn_W1, L1_gnn_b1, L1_gnn_g1, L1_gnn_be1, L1_gnn_W2, L1_gnn_b2, L1_gnn_g2, L1_gnn_be2):
    import jax
    import jax.numpy as jnp

    def _L0_gnn_ref(x, adj, Wg0, bg0, Wg1, bg1, Wih, Whh, bih, bhh):
        import jax, jax.numpy as jnp
        import numpy as np
        B, T, D, H = (64, 1024, 128, 128)
        MAX_SKIP = 4

        def _lstm_last(Wih, Whh, bih, bhh, xs):
            N, _, Hd = xs.shape
            bias = bih + bhh

            def step(carry, x_t):
                h, c = carry
                g = x_t @ Wih.T + h @ Whh.T + bias
                i, f, gg, o = jnp.split(g, 4, axis=-1)
                c = jax.nn.sigmoid(f) * c + jax.nn.sigmoid(i) * jnp.tanh(gg)
                h = jax.nn.sigmoid(o) * jnp.tanh(c)
                return ((h, c), None)
            init = (jnp.zeros((N, Hd), xs.dtype), jnp.zeros((N, Hd), xs.dtype))
            (h_last, _), _ = jax.lax.scan(step, init, jnp.swapaxes(xs, 0, 1))
            return h_last
        h = jax.nn.relu(jnp.einsum('ts,bsh->bth', adj, x @ Wg0 + bg0))
        h = jax.nn.relu(jnp.einsum('ts,bsh->bth', adj, h @ Wg1 + bg1))
        Bv, Tv, Hd = h.shape
        for p in range(1, MAX_SKIP + 1):
            nw = Tv // p
            wins = h[:, :nw * p, :].reshape(Bv * nw, p, Hd)
            last = _lstm_last(Wih[p - 1], Whh[p - 1], bih[p - 1], bhh[p - 1], wins)
            idx = jnp.arange(nw) * p + (p - 1)
            h = h.at[:, idx, :].set(last.reshape(Bv, nw, Hd))
        return h

    def _L1_gnn_ref(features, A, W1, b1, g1, be1, W2, b2, g2, be2):
        import jax, jax.numpy as jnp
        import numpy as np
        EPS = 1e-05

        def _batchnorm(x, gamma, beta):
            mu = jnp.mean(x, axis=0)
            var = jnp.var(x, axis=0)
            return (x - mu) * jax.lax.rsqrt(var + EPS) * gamma + beta
        b, n, d = features.shape
        A_norm = A + jnp.eye(n, dtype=A.dtype)
        deg = jnp.sum(A_norm, axis=0) + jnp.sum(A_norm, axis=1) - jnp.diagonal(A_norm)
        dinv = jax.lax.rsqrt(deg)
        A_hat = A_norm * dinv[:, None] * dinv[None, :]
        agg = jnp.einsum('nm,bmd->bnd', A_hat, features)
        x = agg.reshape(-1, d)
        h = jax.nn.relu(_batchnorm(x @ W1.T + b1, g1, be1))
        out = h @ W2.T + b2
        out = _batchnorm(out, g2, be2)
        return out.reshape(b, n, -1)
    x = _layernorm(x + _L0_gnn_ref(x, adj, L0_gnn_Wg0, L0_gnn_bg0, L0_gnn_Wg1, L0_gnn_bg1, L0_gnn_Wih, L0_gnn_Whh, L0_gnn_bih, L0_gnn_bhh), axis=-1)
    x = _layernorm(x + _L1_gnn_ref(x, adj, L1_gnn_W1, L1_gnn_b1, L1_gnn_g1, L1_gnn_be1, L1_gnn_W2, L1_gnn_b2, L1_gnn_g2, L1_gnn_be2), axis=-1)
    return x

_drawn_inputs = setup_inputs


def setup_inputs(seed=0):
    import zlib

    import numpy as np

    out = dict(_drawn_inputs(seed))
    spreads = {'L0_gnn_bg0': (0.0, 0.8),
     'L0_gnn_bg1': (0.0, 0.8),
     'L1_gnn_b1': (0.0, 0.8),
     'L1_gnn_g1': (1.0, 0.2),
     'L1_gnn_be1': (0.0, 0.1),
     'L1_gnn_b2': (0.0, 0.8),
     'L1_gnn_g2': (1.0, 0.2),
     'L1_gnn_be2': (0.0, 0.1)}
    factors = {'L0_gnn_Wg0': 8.0,
     'L0_gnn_Wg1': 8.0,
     'L0_gnn_Wih': 8.0,
     'L0_gnn_Whh': 8.0,
     'L0_gnn_bih': 2.792,
     'L0_gnn_bhh': 2.807}
    for name, (base, spread) in spreads.items():
        noise = np.random.default_rng([zlib.crc32(name.encode()), seed]).standard_normal(out[name].shape)
        drawn = base * np.exp(spread * noise) if base else spread * noise
        out[name] = jnp.asarray(drawn.astype(out[name].dtype))
    for name, factor in factors.items():
        out[name] = (out[name] * factor).astype(out[name].dtype)
    return out
```

```python
from contextlib import ExitStack

import concourse.bass as bass
from concourse import mybir

F32 = mybir.dt.float32
F32R = mybir.dt.float32r
ALU = mybir.AluOpType
ACT = mybir.ActivationFunctionType
AX = mybir.AxisListType

P = 128
B = 64
T = 128
GB = 4
NT = GB * T
G = B // GB
Q = 4
ITERS = G // Q
HC = 2
EPS = 1e-5
SIG_I, SIG_F, TANH_G, SIG_O = range(4)
FIRST_GATES = (SIG_I, TANH_G, SIG_O)
ALL_GATES = (SIG_F, SIG_I, TANH_G, SIG_O)
WIN = {2: 8, 3: 7, 4: 8}
PAIRS = {p: (T // p) // (2 * WIN[p]) for p in WIN}
for _p in WIN:
    assert PAIRS[_p] * 2 * WIN[_p] == T // _p
NMAT = 6
V_BIH, V_BHH, V_B1, V_G1, V_BE1, V_B2, V_G2, V_BE2, V_END = 0, 16, 32, 34, 36, 38, 39, 40, 41


class Steps:

    def __init__(self, eng, sem, base=0):
        self.eng, self.sem, self.base, self.n = eng, sem, base, 0

    def then(self, ins):
        ins.then_inc(self.sem, 1)
        self.n += 1

    def settle(self):
        self.eng.wait_ge(self.sem, self.base + self.n)


def build(nc, xT_d, mats_d, lw_d, vecs_d, out_d):
    ctx = ExitStack()
    with ctx:
        base = nc.sbuf_base
        KB = 1024
        arena_bytes = 190 * KB
        arena = ctx.enter_context(nc.sbuf_tensor("arena", [P, arena_bytes // 4], F32))
        start = base + (-base) % 32

        def at(name, off_kb, shape, dt=F32):
            size = 4
            for n in shape[1:]:
                size *= n
            assert off_kb * KB + size <= arena_bytes, name
            return nc.alloc_sbuf_tensor_at(name, shape, dt, offset=start + off_kb * KB)

        def sb(name, shape, dt=F32):
            return ctx.enter_context(nc.sbuf_tensor(name, shape, dt))

        hT = at("hT", 0, [P, T, B])
        lw_raw = at("lw_raw", 0, [P, 7, 512])
        h_hi = at("h_hi", 32, [P, T, B], F32R)
        h_lo = at("h_lo", 64, [P, T, B], F32R)
        xt_in = at("xt_in", 96, [P, Q, NT])
        ynat = at("ynat", 104, [P, Q, NT])
        h1T = at("h1T", 112, [P, Q, NT])
        g_lo = at("g_lo", 104, [P, Q, NT], F32R)
        g_hi = at("g_hi", 112, [P, Q, NT], F32R)
        lw_hi = at("lw_hi", 128, [P, 7, 512], F32R)
        lw_lo = at("lw_lo", 142, [P, 7, 512], F32R)
        gi = at("gi", 156, [P, 2, NT])
        gf = at("gf", 160, [P, 2, NT])
        gg = at("gg", 164, [P, 2, NT])
        go = at("go", 168, [P, 2, NT])
        cell = at("cell", 172, [P, 2, NT])
        hbuf = at("hbuf", 176, [P, 2, NT])
        hs_hi = at("hs_hi", 180, [P, 2, NT], F32R)
        hs_lo = at("hs_lo", 184, [P, 2, NT], F32R)
        x_res = at("x_res", 96, [P, B, T])
        h1 = at("h1", 32, [P, HC, G * NT])
        x1 = at("x1", 128, [P, B, P])
        res = at("res", 160, [P, Q, NT])
        x1s = at("x1s", 168, [P, Q, NT])
        aggT = at("aggT", 176, [P, 2, NT])
        hr = at("hr", 180, [P, 2, HC, NT])
        outT = at("outT", 0, [P, G * NT])
        sT = at("sT", 160, [P, Q, NT])
        r2 = at("r2", 168, [P, Q, NT])
        ob = at("ob", 176, [P, Q, NT])

        mats = sb("mats", [P, NMAT * P + 2 * HC * P])
        vecs = sb("vecs", [P, V_END])
        wg0, wg1, adjT, adj, bg0, bg1 = (mats[:, k * P:(k + 1) * P] for k in range(NMAT))
        w1T = mats[:, NMAT * P:(NMAT + HC) * P].rearrange("p (h c) -> p h c", h=HC)
        w2T = mats[:, (NMAT + HC) * P:].rearrange("p (h c) -> p h c", h=HC)
        lbias = sb("lbias", [P, 4, 4])
        ident = sb("ident", [P, P])
        ahatT = sb("ahatT", [P, P])
        anorm = sb("anorm", [P, P])
        dsm = sb("dsm", [P, 8])
        lnst = sb("lnst", [P, Q * GB, 6])
        lnsm = sb("lnsm", [P, 8, Q * GB])
        st1 = sb("st1", [P, HC, G, 6])
        st2 = sb("st2", [P, G, 6])
        mv = sb("mv", [P, 3, 2])
        bnsm = sb("bnsm", [P, 8, 3])
        bank = [ctx.enter_context(nc.psum_tensor(f"bank{i}", [P, NT], F32)) for i in range(8)]

        def sem(name):
            return ctx.enter_context(nc.semaphore(name))

        mats_in, vecs_in, lw_in = sem("mats_in"), sem("vecs_in"), sem("lw_in")
        x_in = [sem(f"x_in{q}") for q in range(Q)]
        ident_step, lw_hi_ready, lw_ready = sem("ident_step"), sem("lw_hi_ready"), sem("lw_ready")
        dve_set, lbias_ready = sem("dve_set"), sem("lbias_ready")
        deg_ready, deg_root, dinv_ready = sem("deg_ready"), sem("deg_root"), sem("dinv_ready")
        drow_ready, ahat_ready = sem("drow_ready"), sem("ahat_ready")
        xw_done, xw_ready = sem("xw_done"), sem("xw_ready")
        ag1_done, h1_ready = sem("ag1_done"), sem("h1_ready")
        hw_done, hw_ready = sem("hw_done"), sem("hw_ready")
        ag2_done, g_hi_ready, g_lo_ready = sem("ag2_done"), sem("g_hi_ready"), sem("g_lo_ready")

        class CellSems:
            def __init__(self, name):
                self.gate_done = sem(f"{name}_gate_done")
                self.gate_read = sem(f"{name}_gate_read")
                self.term = sem(f"{name}_term")
                self.cell_ready = sem(f"{name}_cell")
                self.tanh_ready = sem(f"{name}_tanh")
                self.h_full = sem(f"{name}_h_full")
                self.h_hi = sem(f"{name}_h_hi")
                self.h_ready = sem(f"{name}_h_ready")

        one = CellSems("p1")
        win = {p: [CellSems(f"p{p}s{s}") for s in range(2)] for p in WIN}
        xres_in = sem("xres_in")
        res_ready, res_t_done = sem("res_ready"), sem("res_t_done")
        ln_step, ln_var, ln_sd = sem("ln_step"), sem("ln_var"), sem("ln_sd")
        ln_ready = sem("ln_ready")
        x1_dve, x1_act = sem("x1_dve"), sem("x1_act")
        x1_saved = [sem(f"x1_saved{q}") for q in range(Q)]
        agg_done, agg_ready = sem("agg_done"), sem("agg_ready")
        w1_done, w1_read, st1_done = sem("w1_done"), sem("w1_read"), sem("st1_done")
        bn_step, bn_var, bn_sd, bn_ready = sem("bn_step"), sem("bn_var"), sem("bn_sd"), sem("bn_ready")
        hr_ready, w2_done, w2_read, st2_done = sem("hr_ready"), sem("w2_done"), sem("w2_read"), sem("st2_done")
        sT_ready, sT_t_done, r2_ready = sem("sT_ready"), sem("sT_t_done"), sem("r2_ready")
        ln2_step, ln2_var, ln2_sd = sem("ln2_step"), sem("ln2_var"), sem("ln2_sd")
        out_ready = sem("out_ready")
        out_saved = [sem(f"out_saved{q}") for q in range(Q)]

        ihw = lambda p: p - 1
        hhw = lambda p: 4 + p - 2
        gates_of = lambda p, j: FIRST_GATES if j == 0 else ALL_GATES
        gates_before = lambda j: 0 if j == 0 else 3 + 4 * (j - 1)
        gcols = lambda g: slice(g * P, (g + 1) * P)

        def grp(n):
            return bass.ds(n * NT, NT)

        def windows(buf, p, t0, j):
            return buf[:, bass.ds(t0, p * WIN[p]), :].rearrange("p (w j) b -> p w j b", j=p)[:, :, j, :]

        def tb(ap, p):
            return ap[:, 0:WIN[p] * B].rearrange("p (w b) -> p w b", b=B)

        block = ctx.enter_context(nc.Block())

        @block.sync
        def _(sp):
            sp.dma_start(mats[:, :], mats_d).then_inc(mats_in, 16)

            def load(it, q):
                sp.dma_start(xt_in[:, q, :].rearrange("p (b s) -> p b s", b=GB),
                             xT_d[:, bass.ds(it * (Q * GB) + q * GB, GB), :]).then_inc(x_in[q], 16)

            for q in range(Q):
                load(0, q)
            sp.dma_start(vecs[:, :], vecs_d).then_inc(vecs_in, 16)
            sp.dma_start(lw_raw[:, :, :], lw_d).then_inc(lw_in, 16)
            with sp.Fori(1, ITERS) as it:
                for q in range(Q):
                    sp.wait_ge(xw_done, it * Q + (q - Q + 1))
                    load(it, q)
            sp.wait_ge(one.gate_done, 3 * G)
            sp.dma_start(x_res[:, :, :], xT_d).then_inc(xres_in, 16)
            with sp.Fori(0, ITERS) as it:
                for q in range(Q):
                    made = x1_dve if q % 2 == 0 else x1_act
                    sp.wait_ge(made, it * 2 + (q // 2 + 1))
                    sp.dma_start(x1[:, bass.ds(it * (Q * GB) + q * GB, GB), :],
                                 x1s[:, q, :].rearrange("p (b d) -> p b d", b=GB)).then_inc(x1_saved[q], 16)
            with sp.Fori(0, ITERS) as it:
                for q in range(Q):
                    sp.wait_ge(out_ready, it * Q + (q + 1))
                    sp.dma_start(out_d[:, bass.ds(it * (Q * GB) + q * GB, GB), :],
                                 ob[:, q, :].rearrange("p (b d) -> p b d", b=GB)).then_inc(out_saved[q], 16)
            for q in range(Q):
                sp.wait_ge(out_saved[q], 16 * ITERS)

        @block.gpsimd
        def _(pool):
            nc.gpsimd.memset(ident[:, :], 0.0).then_inc(ident_step, 1)
            pool.wait_ge(ident_step, 1)
            nc.gpsimd.affine_select(out=ident[:, :], in_=ident[:, :], compare_op=ALU.not_equal, fill=1.0,
                                    base=0, pattern=[[-1, P]], channel_multiplier=1).then_inc(ident_step, 1)
            pool.wait_ge(lw_in, 16)
            for k in range(7):
                nc.gpsimd.tensor_copy(lw_hi[:, k, :], lw_raw[:, k, :]).then_inc(lw_hi_ready, 1)
                pool.wait_ge(lw_hi_ready, k + 1)
                nc.gpsimd.tensor_tensor(lw_lo[:, k, :], lw_raw[:, k, :], lw_hi[:, k, :].bitcast(F32),
                                        ALU.subtract).then_inc(lw_ready, 1)
            pool.wait_ge(xres_in, 16)
            for s in range(2):
                pool.wait_ge(win[4][s].h_ready, 4 * PAIRS[4])
            with pool.Fori(0, ITERS) as it:
                for q in range(Q):
                    pool.wait_ge(res_t_done, it * Q)
                    b0 = it * (Q * GB) + q * GB
                    nc.gpsimd.tensor_tensor(
                        res[:, q, :].rearrange("p (b t) -> p b t", b=GB), x_res[:, bass.ds(b0, GB), :],
                        hT[:, :, bass.ds(b0, GB)].rearrange("p t b -> p b t"), ALU.add).then_inc(res_ready, 1)

        @block.tensor
        def _(pe):
            def split_products(out, w, wk, gate, hi, lo, start, stop):
                cols = gcols(gate)
                nc.tensor.matmul(out, w[1][:, wk, cols], hi, start=start, stop=False)
                nc.tensor.matmul(out, w[0][:, wk, cols], lo, start=False, stop=False)
                return nc.tensor.matmul(out, w[0][:, wk, cols], hi, start=False, stop=stop)

            lw = (lw_hi, lw_lo)
            pe.wait_ge(mats_in, 16)
            pe.wait_ge(ident_step, 2)
            pe.wait_ge(dinv_ready, 1)
            nc.tensor.matmul(bank[4][:, 0:P], anorm[:, :], ident[:, :], start=True, stop=True).then_inc(drow_ready, 1)
            pe.wait_ge(ahat_ready, 1)

            def data_stationary(q, data, moving, done):
                for k in range(GB):
                    last = nc.tensor.matmul(bank[q][:, k * P:(k + 1) * P], data[:, q, k * P:(k + 1) * P],
                                            moving, start=True, stop=True)
                last.then_inc(done, 1)

            def one_step(it, q):
                pe.wait_ge(g_lo_ready, it * Q + (q + 1))
                for k, gate in enumerate(FIRST_GATES):
                    m = 3 * q + k
                    pe.wait_ge(one.gate_read, it * (3 * Q) + (m - 3 if m >= 4 else 0))
                    split_products(bank[4 + m % 4][:, :], lw, ihw(1), gate, g_hi[:, q, :], g_lo[:, q, :],
                                   True, True).then_inc(one.gate_done, 1)

            pe.wait_ge(lw_ready, 7)
            with pe.Fori(0, ITERS) as it:
                for q in range(Q):
                    pe.wait_ge(x_in[q], it * 16 + 16)
                    data_stationary(q, xt_in, wg0, xw_done)
                for q in range(Q):
                    pe.wait_ge(xw_ready, it * Q + (q + 1))
                    data_stationary(q, ynat, adjT, ag1_done)
                for q in range(Q):
                    pe.wait_ge(h1_ready, it * Q + (q + 1))
                    data_stationary(q, h1T, wg1, hw_done)
                for q in range(Q):
                    pe.wait_ge(hw_ready, it * Q + (q + 1))
                    data_stationary(q, ynat, adjT, ag2_done)
                    if q == Q - 2:
                        one_step(it, 0)
                for q in range(1, Q):
                    one_step(it, q)

            pe.wait_ge(one.h_ready, G)
            pe.wait_ge(one.gate_read, 3 * G)
            for p in WIN:
                per = gates_before(p)
                if p > 2:
                    for s in range(2):
                        pe.wait_ge(win[p - 1][s].gate_read, gates_before(p - 1) * PAIRS[p - 1])
                with pe.Fori(0, PAIRS[p]) as it:
                    if p > 2:
                        for i in range(PAIRS[p]):
                            need = -(-2 * WIN[p] * p * (i + 1) // (2 * WIN[p - 1] * (p - 1)))
                            assert min(need, PAIRS[p - 1]) <= i + 2 <= PAIRS[p - 1]
                        for s in range(2):
                            pe.wait_ge(win[p - 1][s].h_ready, it * (p - 1) + 2 * (p - 1))
                    for j in range(p):
                        for s in range(2):
                            w = win[p][s]
                            t0 = it * (2 * WIN[p] * p) + s * WIN[p] * p
                            hi, lo = windows(h_hi, p, t0, j), windows(h_lo, p, t0, j)
                            pe.wait_ge(w.gate_read, it * per + gates_before(j))
                            for k, gate in enumerate(gates_of(p, j)):
                                last = split_products(tb(bank[4 * s + k], p), lw, ihw(p), gate, hi, lo,
                                                      True, j == 0)
                                if j == 0:
                                    last.then_inc(w.gate_done, 1)
                            if j:
                                pe.wait_ge(w.h_ready, it * p + j)
                                for k, gate in enumerate(ALL_GATES):
                                    split_products(tb(bank[4 * s + k], p), lw, hhw(p), gate,
                                                   tb(hs_hi[:, s, :], p), tb(hs_lo[:, s, :], p),
                                                   False, True).then_inc(w.gate_done, 1)

            for s in range(2):
                pe.wait_ge(win[4][s].gate_read, gates_before(4) * PAIRS[4])

            def aggregate(it, q):
                pe.wait_ge(x1_dve if q % 2 == 0 else x1_act, it * 2 + (q // 2 + 1))
                pe.wait_ge(agg_ready, it * Q + (q - 1 if q >= 2 else 0))
                for k in range(GB):
                    last = nc.tensor.matmul(bank[4 + q % 2][:, k * P:(k + 1) * P], x1s[:, q, k * P:(k + 1) * P],
                                            ahatT[:, :], start=True, stop=True)
                last.then_inc(agg_done, 1)

            def first_product(it, q):
                pe.wait_ge(agg_ready, it * Q + (q + 1))
                pe.wait_ge(w1_read, it * (HC * Q) + HC * q)
                for h in range(HC):
                    nc.tensor.matmul(bank[6 + h][:, :], w1T[:, h, :], aggT[:, q % 2, :],
                                     start=True, stop=True).then_inc(w1_done, 1)

            with pe.Fori(0, ITERS) as it:
                for q in range(Q):
                    pe.wait_ge(res_ready, it * Q + (q + 1))
                    if q == 0:
                        pe.wait_ge(x1_dve, it * 2)
                        pe.wait_ge(x1_act, it * 2)
                    for k in range(GB):
                        last = nc.tensor.transpose(bank[q][:, k * P:(k + 1) * P],
                                                   res[:, q, k * P:(k + 1) * P], ident[:, :])
                    last.then_inc(res_t_done, 1)
                aggregate(it, 0)
                for q in range(1, Q):
                    aggregate(it, q)
                    first_product(it, q - 1)
                first_product(it, Q - 1)

            with pe.Fori(0, G // 2) as it:
                for s in range(2):
                    pe.wait_ge(hr_ready, it * (2 * HC) + HC * (s + 1))
                    pe.wait_ge(w2_read, it * 2)
                    for h in range(HC):
                        last = nc.tensor.matmul(bank[s][:, :], w2T[:, h, :], hr[:, s, h, :],
                                                start=h == 0, stop=h == HC - 1)
                    last.then_inc(w2_done, 1)

            pe.wait_ge(w2_read, G)
            with pe.Fori(0, ITERS) as it:
                for q in range(Q):
                    pe.wait_ge(sT_ready, it * Q + (q + 1))
                    if q == 0:
                        pe.wait_ge(r2_ready, it * Q)
                    for k in range(GB):
                        last = nc.tensor.transpose(bank[4 + q][:, k * P:(k + 1) * P],
                                                   sT[:, q, k * P:(k + 1) * P], ident[:, :])
                    last.then_inc(sT_t_done, 1)

        @block.scalar
        def _(act):
            act.wait_ge(deg_ready, 1)
            nc.scalar.activation(dsm[:, 4:5], dsm[:, 3:4], ACT.Sqrt).then_inc(deg_root, 1)
            act.wait_ge(lbias_ready, 1)

            def gate(out, src, p, g, done):
                nc.scalar.activation(out, src, ACT.Tanh if g == TANH_G else ACT.Sigmoid,
                                     bias=lbias[:, p - 1, g:g + 1]).then_inc(done, 1)

            gbuf = {SIG_I: gi, SIG_F: gf, TANH_G: gg, SIG_O: go}

            def one_gates(it, q):
                act.wait_ge(one.h_ready, it * Q + (q - 1 if q >= 2 else 0))
                for k, g in enumerate(FIRST_GATES):
                    m = 3 * q + k
                    act.wait_ge(one.gate_done, it * (3 * Q) + m + 1)
                    gate(gbuf[g][:, q % 2, :], bank[4 + m % 4][:, :], 1, g, one.gate_read)

            def one_tanh(it, q):
                act.wait_ge(one.cell_ready, it * Q + (q + 1))
                nc.scalar.activation(gg[:, q % 2, :], cell[:, q % 2, :], ACT.Tanh).then_inc(one.tanh_ready, 1)

            def relu_hi(it, q):
                act.wait_ge(ag2_done, it * Q + (q + 1))
                nc.scalar.activation(g_hi[:, q, :], bank[q][:, :], ACT.Relu).then_inc(g_hi_ready, 1)

            with act.Fori(0, ITERS) as it:
                for q in range(Q):
                    act.wait_ge(ag1_done, it * Q + (q + 1))
                    nc.scalar.activation(h1T[:, q, :], bank[q][:, :], ACT.Relu).then_inc(h1_ready, 1)
                for q in range(Q - 1):
                    relu_hi(it, q)
                one_gates(it, 0)
                relu_hi(it, Q - 1)
                for q in range(1, Q):
                    one_gates(it, q)
                    one_tanh(it, q - 1)
                one_tanh(it, Q - 1)

            def step_gates(it, p, j, s):
                w, n = win[p][s], WIN[p] * B
                if j == 0:
                    act.wait_ge(w.h_ready, it * p)
                for k, g in enumerate(gates_of(p, j)):
                    act.wait_ge(w.gate_done, it * gates_before(p) + (gates_before(j) + k + 1))
                    gate(gbuf[g][:, s, 0:n], bank[4 * s + k][:, 0:n], p, g, w.gate_read)

            def step_tanh(it, p, j, s):
                w, n = win[p][s], WIN[p] * B
                act.wait_ge(w.cell_ready, it * p + (j + 1))
                nc.scalar.activation(gg[:, s, 0:n], cell[:, s, 0:n], ACT.Tanh).then_inc(w.tanh_ready, 1)

            for p in WIN:
                if p == 2:
                    act.wait_ge(one.h_ready, G)
                else:
                    for s in range(2):
                        act.wait_ge(win[p - 1][s].h_ready, (p - 1) * PAIRS[p - 1])
                with act.Fori(0, PAIRS[p]) as it:
                    for s in range(2):
                        step_gates(it, p, 0, s)
                    for s in range(2):
                        step_tanh(it, p, 0, s)
                    for j in range(1, p):
                        for s in range(2):
                            step_gates(it, p, j, s)
                            step_tanh(it, p, j, s)

            def agg_out(it, q):
                act.wait_ge(agg_done, it * Q + (q + 1))
                act.wait_ge(w1_done, it * (HC * Q) + (HC * (q - 1) if q >= 2 else 0))
                nc.scalar.activation(aggT[:, q % 2, :], bank[4 + q % 2][:, :], ACT.Copy).then_inc(agg_ready, 1)

            def w1_out(it, q):
                for h in range(HC):
                    act.wait_ge(w1_done, it * (HC * Q) + (HC * q + h + 1))
                    nc.scalar.activation(h1[:, h, grp(it * Q + q)], bank[6 + h][:, :], ACT.Identity,
                                         bias=vecs[:, V_B1 + h:V_B1 + h + 1]).then_inc(w1_read, 1)

            with act.Fori(0, ITERS) as it:
                act.wait_ge(ln_var, it + 1)
                nc.scalar.activation(lnsm[:, 6, :], lnsm[:, 5, :], ACT.Sqrt).then_inc(ln_sd, 1)
                act.wait_ge(ln_ready, it + 1)
                act.wait_ge(agg_done, it * Q)
                for q in (1, 3):
                    act.wait_ge(x1_saved[q], it * 16)
                    for k in range(GB):
                        c = q * GB + k
                        last = nc.scalar.activation(
                            x1s[:, q, k * P:(k + 1) * P], bank[q][:, k * P:(k + 1) * P], ACT.Identity,
                            bias=lnsm[:, 7, c:c + 1], scale=lnsm[:, 4, c:c + 1])
                    last.then_inc(x1_act, 1)
                agg_out(it, 0)
                for q in range(1, Q):
                    agg_out(it, q)
                    w1_out(it, q - 1)
                w1_out(it, Q - 1)

            act.wait_ge(bn_var, 1)
            nc.scalar.activation(bnsm[:, 1, 0:HC], bnsm[:, 0, 0:HC], ACT.Sqrt).then_inc(bn_sd, 1)
            act.wait_ge(bn_ready, 1)
            with act.Fori(0, G // 2) as it:
                for s in range(2):
                    act.wait_ge(w2_done, it * 2)
                    for h in range(HC):
                        nc.scalar.activation(hr[:, s, h, :], h1[:, h, grp(it * 2 + s)], ACT.Relu,
                                             bias=bnsm[:, 7, h:h + 1], scale=bnsm[:, 6, h:h + 1]
                                             ).then_inc(hr_ready, 1)

            act.wait_ge(bn_var, 2)
            nc.scalar.activation(bnsm[:, 1, 2:3], bnsm[:, 0, 2:3], ACT.Sqrt).then_inc(bn_sd, 1)
            act.wait_ge(bn_ready, 2)
            with act.Fori(0, ITERS) as it:
                for q in range(Q):
                    act.wait_ge(sT_t_done, it * Q)
                    nc.scalar.activation(sT[:, q, :], outT[:, grp(it * Q + q)], ACT.Identity,
                                         bias=bnsm[:, 7, 2:3], scale=bnsm[:, 6, 2:3]).then_inc(sT_ready, 1)
                act.wait_ge(ln2_var, it + 1)
                nc.scalar.activation(lnsm[:, 6, :], lnsm[:, 5, :], ACT.Sqrt).then_inc(ln2_sd, 1)

        @block.vector
        def _(dve):
            V = nc.vector

            def newton(st, v, sd, r, t):
                st.then(V.reciprocal(r, sd))
                st.settle()
                st.then(V.tensor_tensor(t, v, r, ALU.mult))
                st.settle()
                st.then(V.tensor_tensor(t, t, r, ALU.mult))
                st.settle()
                st.then(V.tensor_scalar(t, t, -0.5, 1.5, ALU.mult, ALU.add))
                st.settle()
                st.then(V.tensor_tensor(r, r, t, ALU.mult))
                st.settle()

            st = Steps(dve, dve_set)
            dve.wait_ge(mats_in, 16)
            dve.wait_ge(ident_step, 2)
            st.then(V.tensor_tensor(anorm[:, :], adj, ident[:, :], ALU.add))
            st.then(V.tensor_tensor(ahatT[:, :], adjT, ident[:, :], ALU.add))
            st.settle()
            st.then(V.reduce_sum(dsm[:, 0:1], anorm[:, :], AX.X))
            st.then(V.reduce_sum(dsm[:, 1:2], ahatT[:, :], AX.X))
            st.settle()
            st.then(V.tensor_tensor(anorm[:, :], anorm[:, :], ident[:, :], ALU.mult))
            st.settle()
            st.then(V.reduce_sum(dsm[:, 2:3], anorm[:, :], AX.X))
            st.then(V.tensor_tensor(dsm[:, 1:2], dsm[:, 0:1], dsm[:, 1:2], ALU.add))
            st.settle()
            V.tensor_tensor(dsm[:, 3:4], dsm[:, 1:2], dsm[:, 2:3], ALU.subtract).then_inc(deg_ready, 1)
            dve.wait_ge(deg_root, 1)
            newton(st, dsm[:, 3:4], dsm[:, 4:5], dsm[:, 5:6], dsm[:, 6:7])
            st.then(V.memset(anorm[:, :], 0.0))
            st.settle()
            V.tensor_scalar(anorm[:, :], anorm[:, :], dsm[:, 5:6], None, ALU.add).then_inc(dinv_ready, 1)
            dve.wait_ge(drow_ready, 1)
            V.scalar_tensor_tensor(out=ahatT[:, :], in0=ahatT[:, :], scalar=dsm[:, 5:6],
                                   in1=bank[4][:, 0:P], op0=ALU.mult, op1=ALU.mult).then_inc(ahat_ready, 1)
            dve.wait_ge(vecs_in, 16)
            V.tensor_tensor(lbias[:, :, :].rearrange("p a b -> p (a b)"), vecs[:, V_BIH:V_BHH],
                            vecs[:, V_BHH:V_B1], ALU.add).then_inc(lbias_ready, 1)

            def add_bias(it, q, b, done, ready):
                dve.wait_ge(done, it * Q + (q + 1))
                V.tensor_tensor(ynat[:, q, :].rearrange("p (k c) -> p k c", k=GB),
                                bank[q][:, :].rearrange("p (k c) -> p k c", k=GB),
                                b[:, None, :].to_broadcast([P, GB, P]), ALU.add).then_inc(ready, 1)

            def relu_lo(it, q):
                dve.wait_ge(g_hi_ready, it * Q + (q + 1))
                V.scalar_tensor_tensor(out=g_lo[:, q, :], in0=bank[q][:, :], scalar=0.0,
                                       in1=g_hi[:, q, :].bitcast(F32), op0=ALU.max,
                                       op1=ALU.subtract).then_inc(g_lo_ready, 1)

            def one_cell(it, q):
                dve.wait_ge(one.gate_read, it * (3 * Q) + 3 * (q + 1))
                V.tensor_tensor(cell[:, q % 2, :], gi[:, q % 2, :], gg[:, q % 2, :],
                                ALU.mult).then_inc(one.cell_ready, 1)

            def one_h(it, q):
                b0 = it * (Q * GB) + q * GB

                def place(buf):
                    return buf[:, :, bass.ds(b0, GB)].rearrange("p t b -> p b t")

                def bt(ap):
                    return ap.rearrange("p (b t) -> p b t", b=GB)

                n = it * Q + (q + 1)
                dve.wait_ge(one.tanh_ready, n)
                V.tensor_tensor(place(hT), bt(go[:, q % 2, :]), bt(gg[:, q % 2, :]),
                                ALU.mult).then_inc(one.h_full, 1)
                dve.wait_ge(one.h_full, n)
                V.tensor_copy(place(h_hi), place(hT)).then_inc(one.h_hi, 1)
                dve.wait_ge(one.h_hi, n)
                V.tensor_tensor(place(h_lo), place(hT), place(h_hi).bitcast(F32),
                                ALU.subtract).then_inc(one.h_ready, 1)

            dve.wait_ge(lw_ready, 7)
            with dve.Fori(0, ITERS) as it:
                for q in range(Q):
                    add_bias(it, q, bg0, xw_done, xw_ready)
                for q in range(Q):
                    add_bias(it, q, bg1, hw_done, hw_ready)
                for q in range(Q - 1):
                    relu_lo(it, q)
                one_cell(it, 0)
                relu_lo(it, Q - 1)
                for q in range(1, Q):
                    one_cell(it, q)
                    one_h(it, q - 1)
                one_h(it, Q - 1)

            def step_cell(it, p, j, s):
                w, n = win[p][s], WIN[p] * B
                c, i, f, g = (x[:, s, 0:n] for x in (cell, gi, gf, gg))
                seen = it * gates_before(p) + gates_before(j)
                if j == 0:
                    dve.wait_ge(w.gate_read, seen + 3)
                    V.tensor_tensor(c, i, g, ALU.mult).then_inc(w.cell_ready, 1)
                else:
                    terms = it * (2 * (p - 1)) + 2 * j
                    dve.wait_ge(w.gate_read, seen + 1)
                    V.tensor_tensor(c, f, c, ALU.mult).then_inc(w.term, 1)
                    dve.wait_ge(w.gate_read, seen + 3)
                    V.tensor_tensor(i, i, g, ALU.mult).then_inc(w.term, 1)
                    dve.wait_ge(w.term, terms)
                    V.tensor_tensor(c, c, i, ALU.add).then_inc(w.cell_ready, 1)

            def step_h(it, p, j, s):
                w = win[p][s]
                if j == p - 1:
                    t0 = it * (2 * WIN[p] * p) + s * WIN[p] * p
                    full, hi, lo = (windows(x, p, t0, j) for x in (hT, h_hi, h_lo))
                else:
                    full, hi, lo = (tb(x[:, s, :], p) for x in (hbuf, hs_hi, hs_lo))
                n = it * p + (j + 1)
                dve.wait_ge(w.gate_read, it * gates_before(p) + gates_before(j + 1))
                dve.wait_ge(w.tanh_ready, n)
                V.tensor_tensor(full, tb(go[:, s, :], p), tb(gg[:, s, :], p), ALU.mult).then_inc(w.h_full, 1)
                dve.wait_ge(w.h_full, n)
                V.tensor_copy(hi, full).then_inc(w.h_hi, 1)
                dve.wait_ge(w.h_hi, n)
                V.tensor_tensor(lo, full, hi.bitcast(F32), ALU.subtract).then_inc(w.h_ready, 1)

            for p in WIN:
                with dve.Fori(0, PAIRS[p]) as it:
                    for s in range(2):
                        step_cell(it, p, 0, s)
                    for s in range(2):
                        step_h(it, p, 0, s)
                    for j in range(1, p):
                        for s in range(2):
                            step_cell(it, p, j, s)
                            step_h(it, p, j, s)

            def ln_scalars(st, var_sem, sd_sem, count):
                me, qe, mo, qo = (lnst[:, :, k] for k in (1, 2, 4, 5))
                msum, dif, ssq, t, r, v, sd, nm = (lnsm[:, k, :] for k in range(8))
                st.settle()
                st.then(V.tensor_tensor(msum, me, mo, ALU.add))
                st.then(V.tensor_tensor(dif, me, mo, ALU.subtract))
                st.then(V.tensor_tensor(ssq, qe, qo, ALU.add))
                st.settle()
                st.then(V.tensor_tensor(dif, dif, dif, ALU.mult))
                st.then(V.tensor_scalar(ssq, ssq, 1.0 / P, EPS, ALU.mult, ALU.add))
                st.settle()
                V.scalar_tensor_tensor(out=v, in0=dif, scalar=0.25, in1=ssq, op0=ALU.mult,
                                       op1=ALU.add).then_inc(var_sem, 1)
                dve.wait_ge(sd_sem, count)
                newton(st, v, sd, r, t)
                st.then(V.scalar_tensor_tensor(out=nm, in0=msum, scalar=-0.5, in1=r, op0=ALU.mult,
                                               op1=ALU.mult))
                st.settle()

            LN_STEPS = Q * GB + 5 + 5 + 1
            with dve.Fori(0, ITERS) as it:
                st = Steps(dve, ln_step, it * LN_STEPS)
                dve.wait_ge(x1_act, it * 2)
                for q in range(Q):
                    dve.wait_ge(res_t_done, it * Q + (q + 1))
                    for k in range(GB):
                        st.then(V.bn_stats(lnst[:, q * GB + k, :], bank[q][:, k * P:(k + 1) * P]))
                ln_scalars(st, ln_var, ln_sd, it + 1)
                assert st.n == LN_STEPS
                dve.wait_ge(agg_done, it * Q)
                for q in (0, 2):
                    dve.wait_ge(x1_saved[q], it * 16)
                    for k in range(GB):
                        c = q * GB + k
                        last = V.tensor_scalar(x1s[:, q, k * P:(k + 1) * P], bank[q][:, k * P:(k + 1) * P],
                                               lnsm[:, 4, c:c + 1], lnsm[:, 7, c:c + 1], ALU.mult, ALU.add)
                        if q == 0 and k == 0:
                            last.then_inc(ln_ready, 1)
                        elif k == GB - 1:
                            last.then_inc(x1_dve, 1)
                for q in range(Q):
                    for h in range(HC):
                        dve.wait_ge(w1_read, it * (HC * Q) + (HC * q + h + 1))
                        V.bn_stats(st1[:, h, bass.ds(it * Q + q, 1), :].rearrange("p a s -> p (a s)"),
                                   h1[:, h, grp(it * Q + q)]).then_inc(st1_done, 1)

            def bn_scalars(c0, n, g0, be0, count):
                v, sd, r, t = (bnsm[:, k, c0:c0 + n] for k in range(4))
                scale, shift = (bnsm[:, k, c0:c0 + n] for k in (6, 7))
                mean, var = mv[:, c0:c0 + n, 0], mv[:, c0:c0 + n, 1]
                bst.settle()
                V.tensor_scalar(v, var, EPS, None, ALU.add).then_inc(bn_var, 1)
                dve.wait_ge(bn_sd, count)
                newton(bst, v, sd, r, t)
                bst.then(V.tensor_tensor(scale, r, vecs[:, g0:g0 + n], ALU.mult))
                bst.settle()
                bst.then(V.tensor_tensor(t, mean, scale, ALU.mult))
                bst.settle()
                V.tensor_tensor(shift, vecs[:, be0:be0 + n], t, ALU.subtract).then_inc(bn_ready, 1)

            bst = Steps(dve, bn_step)
            dve.wait_ge(st1_done, HC * G)
            for h in range(HC):
                bst.then(V.bn_aggr(mv[:, h, :], st1[:, h, :, :].rearrange("p a s -> p (a s)")))
            bn_scalars(0, HC, V_G1, V_BE1, 1)

            with dve.Fori(0, G // 2) as it:
                for s in range(2):
                    dve.wait_ge(w2_done, it * 2 + (s + 1))
                    V.tensor_scalar(outT[:, grp(it * 2 + s)], bank[s][:, :], vecs[:, V_B2:V_B2 + 1], None,
                                    ALU.add).then_inc(w2_read, 1)
                    dve.wait_ge(w2_read, it * 2 + (s + 1))
                    V.bn_stats(st2[:, bass.ds(it * 2 + s, 1), :].rearrange("p a s -> p (a s)"),
                               outT[:, grp(it * 2 + s)]).then_inc(st2_done, 1)
            dve.wait_ge(st2_done, G)
            bst.then(V.bn_aggr(mv[:, 2, :], st2[:, :, :].rearrange("p a s -> p (a s)")))
            bn_scalars(2, 1, V_G2, V_BE2, 2)

            with dve.Fori(0, ITERS) as it:
                st = Steps(dve, ln2_step, it * LN_STEPS)
                dve.wait_ge(out_ready, it * Q)
                for q in range(Q):
                    dve.wait_ge(sT_t_done, it * Q + (q + 1))
                    dve.wait_ge(x1_saved[q], 16 * ITERS)
                    V.tensor_tensor(r2[:, q, :].rearrange("p (b d) -> p b d", b=GB),
                                    bank[4 + q][:, :].rearrange("p (b d) -> p b d", b=GB),
                                    x1[:, bass.ds(it * (Q * GB) + q * GB, GB), :], ALU.add).then_inc(r2_ready, 1)
                    dve.wait_ge(r2_ready, it * Q + (q + 1))
                    for k in range(GB):
                        st.then(V.bn_stats(lnst[:, q * GB + k, :], r2[:, q, k * P:(k + 1) * P]))
                ln_scalars(st, ln2_var, ln2_sd, it + 1)
                assert st.n == LN_STEPS
                for q in range(Q):
                    dve.wait_ge(out_saved[q], it * 16)
                    for k in range(GB):
                        c = q * GB + k
                        last = V.tensor_scalar(ob[:, q, k * P:(k + 1) * P], r2[:, q, k * P:(k + 1) * P],
                                               lnsm[:, 4, c:c + 1], lnsm[:, 7, c:c + 1], ALU.mult, ALU.add)
                    last.then_inc(out_ready, 1)


def kernel(x, adj, L0_gnn_Wg0, L0_gnn_bg0, L0_gnn_Wg1, L0_gnn_bg1, L0_gnn_Wih, L0_gnn_Whh, L0_gnn_bih,
           L0_gnn_bhh, L1_gnn_W1, L1_gnn_b1, L1_gnn_g1, L1_gnn_be1, L1_gnn_W2, L1_gnn_b2, L1_gnn_g2,
           L1_gnn_be2):
    import numpy as np
    import concourse.bacc as bacc
    from concourse.bass_utils import run_bass_kernel_spmd

    a = np.asarray
    adj = a(adj)
    row = lambda v: np.broadcast_to(a(v)[None, :], (P, P))
    w2 = a(L1_gnn_W2).T.reshape(HC, P, P).transpose(1, 0, 2).reshape(P, HC * P)
    by_gate = lambda v: a(v).reshape(16, P).T
    chan = lambda v: a(v).reshape(-1, P).T
    wT = lambda w: a(w).transpose(2, 0, 1)
    arrays = {
        "xT": np.ascontiguousarray(a(x).transpose(2, 0, 1)),
        "mats": np.ascontiguousarray(np.concatenate(
            [a(L0_gnn_Wg0), a(L0_gnn_Wg1), adj.T, adj, row(L0_gnn_bg0), row(L0_gnn_bg1),
             a(L1_gnn_W1).T, w2], axis=1)),
        "lw": np.ascontiguousarray(np.concatenate([wT(L0_gnn_Wih), wT(L0_gnn_Whh)[:, 1:]], axis=1)),
        "vecs": np.ascontiguousarray(np.concatenate(
            [by_gate(L0_gnn_bih), by_gate(L0_gnn_bhh), chan(L1_gnn_b1), chan(L1_gnn_g1), chan(L1_gnn_be1),
             chan(L1_gnn_b2), chan(L1_gnn_g2), chan(L1_gnn_be2)], axis=1)),
    }
    nc = bacc.Bacc("TRN2", target_bir_lowering=False, num_devices=1)
    ins = [nc.dram_tensor(k + "_dram", v.shape, F32, kind="ExternalInput").ap() for k, v in arrays.items()]
    out = nc.dram_tensor("out_dram", (T, B, P), F32, kind="ExternalOutput").ap()
    build(nc, *ins, out)
    r = run_bass_kernel_spmd(nc, [{k + "_dram": v for k, v in arrays.items()}], core_ids=[0])
    return np.ascontiguousarray(r.results[0]["out_dram"].transpose(1, 0, 2))
```

```python
from contextlib import ExitStack

import concourse.bass as bass
from concourse import mybir

F32 = mybir.dt.float32
F32R = mybir.dt.float32r
ALU = mybir.AluOpType
ACT = mybir.ActivationFunctionType
AX = mybir.AxisListType

P = 128
B = 64
T = 128
GB = 4
NT = GB * T
G = B // GB
Q = 4
ITERS = G // Q
HC = 2
EPS = 1e-5
SIG_I, SIG_F, TANH_G, SIG_O = range(4)
FIRST_GATES = (SIG_I, TANH_G, SIG_O)
ALL_GATES = (SIG_F, SIG_I, TANH_G, SIG_O)
WIN = {2: 8, 3: 7, 4: 8}
PAIRS = {p: (T // p) // (2 * WIN[p]) for p in WIN}
for _p in WIN:
    assert PAIRS[_p] * 2 * WIN[_p] == T // _p
NMAT = 6
NFIRST = 4
V_BIH, V_BHH, V_B1, V_G1, V_BE1, V_B2, V_G2, V_BE2, V_END = 0, 16, 32, 34, 36, 38, 39, 40, 41


class Steps:

    def __init__(self, eng, sem, base=0):
        self.eng, self.sem, self.base, self.n = eng, sem, base, 0

    def then(self, ins):
        ins.then_inc(self.sem, 1)
        self.n += 1

    def settle(self):
        self.eng.wait_ge(self.sem, self.base + self.n)


class Flag:

    def __init__(self, sem, ahead=0):
        self.sem, self.ahead = sem, ahead

    def at(self, rounds, n):
        return rounds + (n + self.ahead)


def build(nc, xT_d, mats_d, lw_d, vecs_d, out_d):
    ctx = ExitStack()
    with ctx:
        base = nc.sbuf_base
        KB = 1024
        arena_bytes = 198 * KB
        ctx.enter_context(nc.sbuf_tensor("arena", [P, arena_bytes // 4], F32))
        start = base + (-base) % 32

        def at(name, off_kb, shape, dt=F32):
            size = 4
            for n in shape[1:]:
                size *= n
            assert off_kb * KB + size <= arena_bytes, name
            return nc.alloc_sbuf_tensor_at(name, shape, dt, offset=start + off_kb * KB)

        def sb(name, shape, dt=F32):
            return ctx.enter_context(nc.sbuf_tensor(name, shape, dt))

        hT = at("hT", 0, [P, B, T])
        h_hi = at("h_hi", 32, [P, T, B], F32R)
        h_lo = at("h_lo", 64, [P, T, B], F32R)
        xt_in = at("xt_in", 96, [P, Q, NT])
        ynat = at("ynat", 104, [P, Q, NT])
        h1T = at("h1T", 112, [P, Q, NT])
        g_hi = at("g_hi", 120, [P, Q, NT], F32R)
        g_lo = at("g_lo", 190, [P, Q, NT], F32R)
        lw_hi = at("lw_hi", 128, [P, 7, 512], F32R)
        lw_lo = at("lw_lo", 142, [P, 7, 512], F32R)
        gi = at("gi", 156, [P, 2, NT])
        gf = at("gf", 160, [P, 2, NT])
        gg = at("gg", 164, [P, 2, NT])
        go = at("go", 168, [P, 2, NT])
        cell = at("cell", 172, [P, 2, NT])
        lw_raw = at("lw_raw", 176, [P, 7, 512])
        hbuf = at("hbuf", 176, [P, 2, NT])
        hs_hi = at("hs_hi", 180, [P, 2, NT], F32R)
        hs_lo = at("hs_lo", 184, [P, 2, NT], F32R)
        x_res = at("x_res", 96, [P, B, T])
        h1 = at("h1", 32, [P, HC, G * NT])
        x1 = at("x1", 128, [P, B, P])
        res = at("res", 160, [P, Q, NT])
        x1s = at("x1s", 168, [P, Q, NT])
        aggT = at("aggT", 176, [P, Q, NT])
        hr = at("hr", 160, [P, Q, HC, NT])
        outT = at("outT", 0, [P, G * NT])
        sT = at("sT", 176, [P, Q, NT])

        mats = sb("mats", [P, NMAT * P + 2 * HC * P])
        vecs = sb("vecs", [P, V_END])
        wg0, bg0, adjT, adj, wg1, bg1 = (mats[:, k * P:(k + 1) * P] for k in range(NMAT))
        w1T = mats[:, NMAT * P:(NMAT + HC) * P].rearrange("p (h c) -> p h c", h=HC)
        w2T = mats[:, (NMAT + HC) * P:].rearrange("p (h c) -> p h c", h=HC)
        lbias = sb("lbias", [P, 4, 4])
        ident = sb("ident", [P, P])
        ahatT = sb("ahatT", [P, P])
        anorm = sb("anorm", [P, P])
        dsm = sb("dsm", [P, 8])
        lnst = sb("lnst", [P, Q * GB, 6])
        lnsm = sb("lnsm", [P, 8, Q * GB])
        st1 = sb("st1", [P, HC, G, 6])
        st2 = sb("st2", [P, G, 6])
        mv = sb("mv", [P, 3, 2])
        bnsm = sb("bnsm", [P, 8, 3])
        bank = [ctx.enter_context(nc.psum_tensor(f"bank{i}", [P, NT], F32)) for i in range(8)]

        def sem(name):
            return ctx.enter_context(nc.semaphore(name))

        first_in, mats_in, vecs_in, lw_in = sem("first_in"), sem("mats_in"), sem("vecs_in"), sem("lw_in")
        x_in = [sem(f"x_in{q}") for q in range(Q)]
        ident_step, lw_hi_ready, lw_ready = sem("ident_step"), sem("lw_hi_ready"), sem("lw_ready")
        dve_set, lbias_ready = sem("dve_set"), sem("lbias_ready")
        deg_ready, deg_root, dinv_ready = sem("deg_ready"), sem("deg_root"), sem("dinv_ready")
        drow_ready, ahat_ready = sem("drow_ready"), sem("ahat_ready")
        xw_done, xw_ready = sem("xw_done"), sem("xw_ready")
        ag1_done, h1_ready = sem("ag1_done"), sem("h1_ready")
        hw_done, hw_ready = sem("hw_done"), sem("hw_ready")
        ag2_done, g_hi_ready, g_lo_ready = sem("ag2_done"), sem("g_hi_ready"), sem("g_lo_ready")

        class CellFlags:
            def __init__(self, name, banks, slots):
                self.gate_done = sem(f"{name}_gate_done")
                self.gate_read = Flag(sem(f"{name}_gate_read"), banks)
                self.term = sem(f"{name}_term")
                self.cell_ready = sem(f"{name}_cell")
                self.tanh_ready = sem(f"{name}_tanh")
                self.h_full = sem(f"{name}_h_full")
                self.h_hi = sem(f"{name}_h_hi")
                self.h_ready = Flag(sem(f"{name}_h_ready"), slots)

        one = CellFlags("p1", 4, 2)
        win = {p: [CellFlags(f"p{p}s{s}", 1, 1) for s in range(2)] for p in WIN}
        xres_in, early_sum = sem("xres_in"), sem("early_sum")
        res_in = [sem(f"res_in{q}") for q in range(Q)]
        res_t_done = sem("res_t_done")
        ln_step, ln_var, ln_sd, ln_ready = sem("ln_step"), sem("ln_var"), sem("ln_sd"), sem("ln_ready")
        x1_dve, x1_act = sem("x1_dve"), sem("x1_act")
        x1_saved = [sem(f"x1_saved{q}") for q in range(Q)]
        agg_done, agg_ready = sem("agg_done"), Flag(sem("agg_ready"), 2)
        w1_done, w1_read, st1_done = sem("w1_done"), Flag(sem("w1_read"), HC), sem("st1_done")
        bn_step, bn_var, bn_sd, bn_ready = sem("bn_step"), sem("bn_var"), sem("bn_sd"), sem("bn_ready")
        hr_ready, w2_done = sem("hr_ready"), Flag(sem("w2_done"), Q)
        w2_read, st2_done = Flag(sem("w2_read"), Q), sem("st2_done")
        sT_ready, sT_t_done, r2_ready = sem("sT_ready"), Flag(sem("sT_t_done"), Q), Flag(sem("r2_ready"), Q)
        ln2_step, ln2_var, ln2_sd, ln2_ready = sem("ln2_step"), sem("ln2_var"), sem("ln2_sd"), sem("ln2_ready")
        out_act, out_dve, out_saved = Flag(sem("out_act"), 1), sem("out_dve"), sem("out_saved")

        ihw = lambda p: p - 1
        hhw = lambda p: 4 + p - 2
        gates_of = lambda p, j: FIRST_GATES if j == 0 else ALL_GATES
        gates_before = lambda j: 0 if j == 0 else 3 + 4 * (j - 1)
        gcols = lambda g: slice(g * P, (g + 1) * P)

        def grp(n):
            return bass.ds(n * NT, NT)

        def batches(it, q):
            return bass.ds(it * (Q * GB) + q * GB, GB)

        def tile_start(p, it, s):
            return it * (2 * WIN[p] * p) + s * WIN[p] * p

        def windows(buf, p, it, s, j):
            return buf[:, bass.ds(tile_start(p, it, s), p * WIN[p]), :].rearrange(
                "p (w j) b -> p w j b", j=p)[:, :, j, :]

        def windows_bt(buf, p, it, s, j):
            return buf[:, :, bass.ds(tile_start(p, it, s), p * WIN[p])].rearrange(
                "p b (w j) -> p w j b", j=p)[:, :, j, :]

        def tb(ap, p):
            return ap[:, 0:WIN[p] * B].rearrange("p (w b) -> p w b", b=B)

        def steps_of_pair(p, it, before):
            for j in range(p):
                yield p, it, j, 0
                if j:
                    yield p, it, j - 1, 1
                elif before:
                    yield before

        block = ctx.enter_context(nc.Block())

        @block.sync
        def _(sp):
            sp.dma_start(mats[:, 0:NFIRST * P], mats_d[:, 0:NFIRST * P]).then_inc(first_in, 16)

            def load(it, q):
                sp.dma_start(xt_in[:, q, :].rearrange("p (b s) -> p b s", b=GB),
                             xT_d[:, batches(it, q), :]).then_inc(x_in[q], 16)

            for q in range(Q):
                load(0, q)
            sp.dma_start(mats[:, NFIRST * P:], mats_d[:, NFIRST * P:]).then_inc(mats_in, 16)
            sp.dma_start(vecs[:, :], vecs_d).then_inc(vecs_in, 16)
            sp.dma_start(lw_raw[:, :, :], lw_d).then_inc(lw_in, 16)
            with sp.Fori(1, ITERS) as it:
                for q in range(Q):
                    sp.wait_ge(xw_done, it * Q + (q + 1 - Q))
                    load(it, q)
            sp.wait_ge(one.gate_done, 3 * G)
            sp.dma_start(x_res[:, :, :], xT_d).then_inc(xres_in, 16)

            def stage(it, q):
                sp.dma_start(res[:, q, :].rearrange("p (b t) -> p b t", b=GB),
                             x_res[:, batches(it, q), :]).then_inc(res_in[q], 16)

            def save(it, q):
                made, n = (x1_dve, q // 2) if q % 2 == 0 else (x1_act, q // 2)
                sp.wait_ge(made, it * 2 + (n + 1))
                sp.dma_start(x1[:, batches(it, q), :],
                             x1s[:, q, :].rearrange("p (b d) -> p b d", b=GB)).then_inc(x1_saved[q], 16)

            sp.wait_ge(early_sum, 8)
            for s in range(2):
                sp.wait_ge(win[4][s].h_ready.sem, win[4][s].h_ready.at(0, 4 * PAIRS[4]))
            for q in range(Q):
                stage(0, q)
            with sp.Fori(1, ITERS) as it:
                for q in range(Q):
                    sp.wait_ge(res_t_done, it * Q + (q + 1 - Q))
                    stage(it, q)
                for q in range(Q):
                    save(it - 1, q)
            for q in range(Q):
                save(ITERS - 1, q)

            with sp.Fori(0, ITERS) as it:
                for q in range(Q):
                    if q < Q - 1:
                        sp.wait_ge(out_act.sem, out_act.at(it * (Q - 1), q + 1))
                    else:
                        sp.wait_ge(out_dve, it + 1)
                    sp.dma_start(out_d[:, batches(it, q), :], x1[:, batches(it, q), :]).then_inc(out_saved, 16)
            sp.wait_ge(out_saved, 16 * G)

        @block.gpsimd
        def _(pool):
            nc.gpsimd.memset(ident[:, :], 0.0).then_inc(ident_step, 1)
            pool.wait_ge(ident_step, 1)
            nc.gpsimd.affine_select(out=ident[:, :], in_=ident[:, :], compare_op=ALU.not_equal, fill=1.0,
                                    base=0, pattern=[[-1, P]], channel_multiplier=1).then_inc(ident_step, 1)
            pool.wait_ge(lw_in, 16)
            for k in range(7):
                nc.gpsimd.tensor_copy(lw_hi[:, k, :], lw_raw[:, k, :]).then_inc(lw_hi_ready, 1)
                pool.wait_ge(lw_hi_ready, k + 1)
                nc.gpsimd.tensor_tensor(lw_lo[:, k, :], lw_raw[:, k, :], lw_hi[:, k, :].bitcast(F32),
                                        ALU.subtract).then_inc(lw_ready, 1)
            pool.wait_ge(xres_in, 16)
            for s in range(2):
                f = win[3][s].h_ready
                pool.wait_ge(f.sem, f.at(0, 3 * PAIRS[3]))
            with pool.Fori(0, 8) as it:
                def early(buf):
                    return buf[:, bass.ds(it * 8, 8), :].rearrange("p b (w j) -> p b w j", j=4)[:, :, :, 0:3]

                nc.gpsimd.tensor_tensor(early(x_res), early(x_res), early(hT), ALU.add).then_inc(early_sum, 1)

        @block.tensor
        def _(pe):
            for f in (w2_done, sT_t_done):
                pe.sem_inc(f.sem, f.ahead)

            def split_products(out, wk, gate, hi, lo, start, stop):
                cols = gcols(gate)
                nc.tensor.matmul(out, lw_lo[:, wk, cols], hi, start=start, stop=False)
                nc.tensor.matmul(out, lw_hi[:, wk, cols], lo, start=False, stop=False)
                return nc.tensor.matmul(out, lw_hi[:, wk, cols], hi, start=False, stop=stop)

            def data_stationary(q, data, moving, done):
                for k in range(GB):
                    last = nc.tensor.matmul(bank[q][:, k * P:(k + 1) * P], data[:, q, k * P:(k + 1) * P],
                                            moving, start=True, stop=True)
                last.then_inc(done, 1)

            def one_step(it, q):
                pe.wait_ge(g_lo_ready, it * Q + (q + 1))
                for k, gate in enumerate(FIRST_GATES):
                    m = 3 * q + k
                    pe.wait_ge(one.gate_read.sem, one.gate_read.at(it * (3 * Q), m - 3))
                    split_products(bank[4 + m % 4][:, :], ihw(1), gate, g_hi[:, q, :], g_lo[:, q, :],
                                   True, True).then_inc(one.gate_done, 1)

            def graph_round(it, first):
                if not first:
                    one_step(it - 1, 0)
                for q in range(Q):
                    pe.wait_ge(x_in[q], it * 16 + 16)
                    if not first:
                        pe.wait_ge(g_lo_ready, it * Q + (q + 1 - Q))
                    data_stationary(q, xt_in, wg0, xw_done)
                if not first:
                    one_step(it - 1, 1)
                for q in range(Q):
                    pe.wait_ge(xw_ready, it * Q + (q + 1))
                    data_stationary(q, ynat, adjT, ag1_done)
                if first:
                    pe.wait_ge(ident_step, 2)
                    pe.wait_ge(dinv_ready, 1)
                    nc.tensor.matmul(bank[4][:, 0:P], anorm[:, :], ident[:, :],
                                     start=True, stop=True).then_inc(drow_ready, 1)
                    pe.wait_ge(mats_in, 16)
                else:
                    one_step(it - 1, 2)
                for q in range(Q):
                    pe.wait_ge(h1_ready, it * Q + (q + 1))
                    data_stationary(q, h1T, wg1, hw_done)
                if not first:
                    one_step(it - 1, 3)
                for q in range(Q):
                    pe.wait_ge(hw_ready, it * Q + (q + 1))
                    data_stationary(q, ynat, adjT, ag2_done)

            pe.wait_ge(first_in, 16)
            graph_round(0, True)
            pe.wait_ge(ahat_ready, 1)
            pe.wait_ge(lw_ready, 7)
            with pe.Fori(1, ITERS) as it:
                graph_round(it, False)
            for q in range(Q):
                one_step(ITERS - 1, q)

            pe.wait_ge(one.h_ready.sem, one.h_ready.at(0, G))
            pe.wait_ge(one.gate_read.sem, one.gate_read.at(0, 3 * G))

            def window_step(p, it, j, s):
                w = win[p][s]
                if p > 2 and j == 0:
                    for i in range(PAIRS[p]):
                        need = -(-2 * WIN[p] * p * (i + 1) // (2 * WIN[p - 1] * (p - 1)))
                        assert min(need, PAIRS[p - 1]) <= i + 2 <= PAIRS[p - 1]
                    for f in (win[p - 1][0].h_ready, win[p - 1][1].h_ready):
                        pe.wait_ge(f.sem, f.at(it * (p - 1), 2 * (p - 1)))
                    if isinstance(it, int):
                        f = win[p - 1][s].gate_read
                        pe.wait_ge(f.sem, f.at(0, gates_before(p - 1) * PAIRS[p - 1]))
                hi, lo = (windows(x, p, it, s, j) for x in (h_hi, h_lo))
                pe.wait_ge(w.gate_read.sem, w.gate_read.at(it * gates_before(p), gates_before(j)))
                for k, gate in enumerate(gates_of(p, j)):
                    last = split_products(tb(bank[4 * s + k], p), ihw(p), gate, hi, lo, True, j == 0)
                    if j == 0:
                        last.then_inc(w.gate_done, 1)
                if j:
                    pe.wait_ge(w.h_ready.sem, w.h_ready.at(it * p, j))
                    for k, gate in enumerate(ALL_GATES):
                        split_products(tb(bank[4 * s + k], p), hhw(p), gate, tb(hs_hi[:, s, :], p),
                                       tb(hs_lo[:, s, :], p), False, True).then_inc(w.gate_done, 1)

            for p in WIN:
                for step in steps_of_pair(p, 0, (p - 1, PAIRS[p - 1] - 1, p - 2, 1) if p > 2 else None):
                    window_step(*step)
                with pe.Fori(1, PAIRS[p]) as it:
                    for step in steps_of_pair(p, it, (p, it - 1, p - 1, 1)):
                        window_step(*step)
            window_step(4, PAIRS[4] - 1, 3, 1)

            for s in range(2):
                f = win[4][s].gate_read
                pe.wait_ge(f.sem, f.at(0, gates_before(4) * PAIRS[4]))

            def to_nat(it, q):
                pe.wait_ge(res_in[q], it * 16 + 16)
                for k in range(GB):
                    last = nc.tensor.transpose(bank[q][:, k * P:(k + 1) * P],
                                               res[:, q, k * P:(k + 1) * P], ident[:, :])
                last.then_inc(res_t_done, 1)

            def aggregate(it, q):
                pe.wait_ge(x1_dve if q % 2 == 0 else x1_act, it * 2 + (q // 2 + 1))
                pe.wait_ge(agg_ready.sem, agg_ready.at(it * Q, q - 1))
                for k in range(GB):
                    last = nc.tensor.matmul(bank[4 + q % 2][:, k * P:(k + 1) * P], x1s[:, q, k * P:(k + 1) * P],
                                            ahatT[:, :], start=True, stop=True)
                last.then_inc(agg_done, 1)

            def first_products(it):
                for q in range(Q):
                    pe.wait_ge(agg_ready.sem, agg_ready.at(it * Q, q + 1))
                    for h in range(HC):
                        pe.wait_ge(w1_read.sem, w1_read.at(it * (HC * Q), HC * (q - 1) + h + 1))
                        nc.tensor.matmul(bank[6 + h][:, :], w1T[:, h, :], aggT[:, q, :],
                                         start=True, stop=True).then_inc(w1_done, 1)

            for q in range(Q):
                to_nat(0, q)
            with pe.Fori(1, ITERS) as it:
                for q in range(Q):
                    aggregate(it - 1, q)
                    to_nat(it, q)
                first_products(it - 1)
            for q in range(Q):
                aggregate(ITERS - 1, q)
            first_products(ITERS - 1)

            with pe.Fori(0, ITERS) as it:
                for q in range(Q):
                    pe.wait_ge(w2_read.sem, w2_read.at(it * Q, q + 1 - Q))
                    for h in range(HC):
                        pe.wait_ge(hr_ready, it * (HC * Q) + (HC * q + h + 1))
                        last = nc.tensor.matmul(bank[q][:, :], w2T[:, h, :], hr[:, q, h, :],
                                                start=h == 0, stop=h == HC - 1)
                    last.then_inc(w2_done.sem, 1)

            with pe.Fori(0, ITERS) as it:
                for q in range(Q):
                    pe.wait_ge(sT_ready, it * Q + (q + 1))
                    pe.wait_ge(r2_ready.sem, r2_ready.at(it * Q, q + 1 - Q))
                    for k in range(GB):
                        last = nc.tensor.transpose(bank[4 + q][:, k * P:(k + 1) * P],
                                                   sT[:, q, k * P:(k + 1) * P], ident[:, :])
                    last.then_inc(sT_t_done.sem, 1)

        @block.scalar
        def _(act):
            for f in [one.gate_read, agg_ready, w1_read, out_act] + [w.gate_read for p in WIN for w in win[p]]:
                act.sem_inc(f.sem, f.ahead)
            act.wait_ge(deg_ready, 1)
            nc.scalar.activation(dsm[:, 4:5], dsm[:, 3:4], ACT.Sqrt).then_inc(deg_root, 1)

            def gate(out, src, p, g, done):
                nc.scalar.activation(out, src, ACT.Tanh if g == TANH_G else ACT.Sigmoid,
                                     bias=lbias[:, p - 1, g:g + 1]).then_inc(done.sem, 1)

            gbuf = {SIG_I: gi, SIG_F: gf, TANH_G: gg, SIG_O: go}

            def one_step(it, q):
                act.wait_ge(one.h_ready.sem, one.h_ready.at(it * Q, q - 1))
                for k, g in enumerate(FIRST_GATES):
                    m = 3 * q + k
                    act.wait_ge(one.gate_done, it * (3 * Q) + (m + 1))
                    gate(gbuf[g][:, q % 2, :], bank[4 + m % 4][:, :], 1, g, one.gate_read)
                act.wait_ge(one.cell_ready, it * Q + (q + 1))
                nc.scalar.activation(gg[:, q % 2, :], cell[:, q % 2, :], ACT.Tanh).then_inc(one.tanh_ready, 1)

            def graph_round(it, first):
                if not first:
                    one_step(it - 1, 0)
                    one_step(it - 1, 1)
                for q in range(Q):
                    act.wait_ge(ag1_done, it * Q + (q + 1))
                    nc.scalar.activation(h1T[:, q, :], bank[q][:, :], ACT.Relu).then_inc(h1_ready, 1)
                if not first:
                    one_step(it - 1, 2)
                    one_step(it - 1, 3)
                for q in range(Q):
                    act.wait_ge(ag2_done, it * Q + (q + 1))
                    nc.scalar.activation(g_hi[:, q, :], bank[q][:, :], ACT.Relu).then_inc(g_hi_ready, 1)

            graph_round(0, True)
            act.wait_ge(lbias_ready, 1)
            with act.Fori(1, ITERS) as it:
                graph_round(it, False)
            for q in range(Q):
                one_step(ITERS - 1, q)

            def window_step(p, it, j, s):
                w, n = win[p][s], WIN[p] * B
                if j == 0:
                    act.wait_ge(w.h_ready.sem, w.h_ready.at(it * p, 0))
                    if p > 2 and isinstance(it, int):
                        f = win[p - 1][s].h_ready
                        act.wait_ge(f.sem, f.at(0, (p - 1) * PAIRS[p - 1]))
                for k, g in enumerate(gates_of(p, j)):
                    act.wait_ge(w.gate_done, it * gates_before(p) + (gates_before(j) + k + 1))
                    gate(gbuf[g][:, s, 0:n], bank[4 * s + k][:, 0:n], p, g, w.gate_read)
                act.wait_ge(w.cell_ready, it * p + (j + 1))
                nc.scalar.activation(gg[:, s, 0:n], cell[:, s, 0:n], ACT.Tanh).then_inc(w.tanh_ready, 1)

            act.wait_ge(one.h_ready.sem, one.h_ready.at(0, G))
            for p in WIN:
                for step in steps_of_pair(p, 0, (p - 1, PAIRS[p - 1] - 1, p - 2, 1) if p > 2 else None):
                    window_step(*step)
                with act.Fori(1, PAIRS[p]) as it:
                    for step in steps_of_pair(p, it, (p, it - 1, p - 1, 1)):
                        window_step(*step)
            window_step(4, PAIRS[4] - 1, 3, 1)

            def agg_out(it):
                for q in range(Q):
                    act.wait_ge(agg_done, it * Q + (q + 1))
                    nc.scalar.activation(aggT[:, q, :], bank[4 + q % 2][:, :], ACT.Copy).then_inc(agg_ready.sem, 1)

            def w1_out(it, q):
                for h in range(HC):
                    act.wait_ge(w1_done, it * (HC * Q) + (HC * q + h + 1))
                    nc.scalar.activation(h1[:, h, grp(it * Q + q)], bank[6 + h][:, :], ACT.Identity,
                                         bias=vecs[:, V_B1 + h:V_B1 + h + 1]).then_inc(w1_read.sem, 1)

            def ln_root(it, var, sd):
                act.wait_ge(var, it + 1)
                nc.scalar.activation(lnsm[:, 6, :], lnsm[:, 5, :], ACT.Sqrt).then_inc(sd, 1)

            def normalise(it, q, first):
                act.wait_ge(ln_ready, it + 1)
                if not first:
                    act.wait_ge(agg_done, it * Q + (q + 1 - Q))
                    act.wait_ge(x1_saved[q], it * 16)
                for k in range(GB):
                    c = q * GB + k
                    last = nc.scalar.activation(
                        x1s[:, q, k * P:(k + 1) * P], bank[q][:, k * P:(k + 1) * P], ACT.Identity,
                        bias=lnsm[:, 7, c:c + 1], scale=lnsm[:, 4, c:c + 1])
                last.then_inc(x1_act, 1)

            ln_root(0, ln_var, ln_sd)
            normalise(0, 1, True)
            normalise(0, 3, True)
            with act.Fori(1, ITERS) as it:
                agg_out(it - 1)
                ln_root(it, ln_var, ln_sd)
                w1_out(it - 1, 0)
                normalise(it, 1, False)
                w1_out(it - 1, 1)
                normalise(it, 3, False)
                w1_out(it - 1, 2)
                w1_out(it - 1, 3)
            agg_out(ITERS - 1)
            for q in range(Q):
                w1_out(ITERS - 1, q)

            act.wait_ge(bn_var, 1)
            nc.scalar.activation(bnsm[:, 1, 0:HC], bnsm[:, 0, 0:HC], ACT.Sqrt).then_inc(bn_sd, 1)
            act.wait_ge(bn_ready, 1)
            for q in range(Q):
                act.wait_ge(x1_saved[q], 16 * ITERS)
            with act.Fori(0, ITERS) as it:
                for q in range(Q):
                    act.wait_ge(w2_done.sem, w2_done.at(it * Q, q + 1 - Q))
                    for h in range(HC):
                        nc.scalar.activation(hr[:, q, h, :], h1[:, h, grp(it * Q + q)], ACT.Relu,
                                             bias=bnsm[:, 7, h:h + 1], scale=bnsm[:, 6, h:h + 1]
                                             ).then_inc(hr_ready, 1)

            act.wait_ge(bn_var, 2)
            nc.scalar.activation(bnsm[:, 1, 2:3], bnsm[:, 0, 2:3], ACT.Sqrt).then_inc(bn_sd, 1)
            act.wait_ge(bn_ready, 2)

            def bn2(it):
                for q in range(Q):
                    act.wait_ge(sT_t_done.sem, sT_t_done.at(it * Q, q + 1 - Q))
                    nc.scalar.activation(sT[:, q, :], outT[:, grp(it * Q + q)], ACT.Identity,
                                         bias=bnsm[:, 7, 2:3], scale=bnsm[:, 6, 2:3]).then_inc(sT_ready, 1)

            def finish(it):
                act.wait_ge(ln2_ready, it + 1)
                for q in range(Q - 1):
                    for k in range(GB):
                        c = q * GB + k
                        b = x1[:, bass.ds(it * (Q * GB) + c, 1), :].rearrange("p b d -> p (b d)")
                        last = nc.scalar.activation(b, b, ACT.Identity, bias=lnsm[:, 7, c:c + 1],
                                                    scale=lnsm[:, 4, c:c + 1])
                    last.then_inc(out_act.sem, 1)

            bn2(0)
            with act.Fori(0, ITERS - 1) as it:
                ln_root(it, ln2_var, ln2_sd)
                bn2(it + 1)
                finish(it)
            ln_root(ITERS - 1, ln2_var, ln2_sd)
            finish(ITERS - 1)

        @block.vector
        def _(dve):
            V = nc.vector
            for f in [one.h_ready, w2_read, r2_ready] + [w.h_ready for p in WIN for w in win[p]]:
                dve.sem_inc(f.sem, f.ahead)

            def newton(st, v, sd, r, t):
                st.then(V.reciprocal(r, sd))
                st.settle()
                st.then(V.tensor_tensor(t, v, r, ALU.mult))
                st.settle()
                st.then(V.tensor_tensor(t, t, r, ALU.mult))
                st.settle()
                st.then(V.tensor_scalar(t, t, -0.5, 1.5, ALU.mult, ALU.add))
                st.settle()
                st.then(V.tensor_tensor(r, r, t, ALU.mult))
                st.settle()

            set_up = Steps(dve, dve_set)

            def degrees(st):
                dve.wait_ge(ident_step, 2)
                st.then(V.tensor_tensor(anorm[:, :], adj, ident[:, :], ALU.add))
                st.then(V.tensor_tensor(ahatT[:, :], adjT, ident[:, :], ALU.add))
                st.settle()
                st.then(V.reduce_sum(dsm[:, 0:1], anorm[:, :], AX.X))
                st.then(V.reduce_sum(dsm[:, 1:2], ahatT[:, :], AX.X))
                st.settle()
                st.then(V.tensor_tensor(anorm[:, :], anorm[:, :], ident[:, :], ALU.mult))
                st.settle()
                st.then(V.reduce_sum(dsm[:, 2:3], anorm[:, :], AX.X))
                st.then(V.tensor_tensor(dsm[:, 1:2], dsm[:, 0:1], dsm[:, 1:2], ALU.add))
                st.settle()
                V.tensor_tensor(dsm[:, 3:4], dsm[:, 1:2], dsm[:, 2:3], ALU.subtract).then_inc(deg_ready, 1)

            def degree_roots(st):
                dve.wait_ge(deg_root, 1)
                newton(st, dsm[:, 3:4], dsm[:, 4:5], dsm[:, 5:6], dsm[:, 6:7])
                st.then(V.memset(anorm[:, :], 0.0))
                st.settle()
                V.tensor_scalar(anorm[:, :], anorm[:, :], dsm[:, 5:6], None, ALU.add).then_inc(dinv_ready, 1)

            def scale_adjacency():
                dve.wait_ge(drow_ready, 1)
                V.scalar_tensor_tensor(out=ahatT[:, :], in0=ahatT[:, :], scalar=dsm[:, 5:6],
                                       in1=bank[4][:, 0:P], op0=ALU.mult, op1=ALU.mult).then_inc(ahat_ready, 1)
                dve.wait_ge(vecs_in, 16)
                V.tensor_tensor(lbias[:, :, :].rearrange("p a b -> p (a b)"), vecs[:, V_BIH:V_BHH],
                                vecs[:, V_BHH:V_B1], ALU.add).then_inc(lbias_ready, 1)

            def add_bias(it, q, b, done, ready):
                dve.wait_ge(done, it * Q + (q + 1))
                V.tensor_tensor(ynat[:, q, :].rearrange("p (k c) -> p k c", k=GB),
                                bank[q][:, :].rearrange("p (k c) -> p k c", k=GB),
                                b[:, None, :].to_broadcast([P, GB, P]), ALU.add).then_inc(ready, 1)

            def one_step(it, q):
                n = it * Q + (q + 1)
                dve.wait_ge(one.gate_read.sem, one.gate_read.at(it * (3 * Q), 3 * (q + 1)))
                V.tensor_tensor(cell[:, q % 2, :], gi[:, q % 2, :], gg[:, q % 2, :],
                                ALU.mult).then_inc(one.cell_ready, 1)

                def parts(buf):
                    return buf[:, :, batches(it, q)].rearrange("p t b -> p b t")

                def bt(ap):
                    return ap.rearrange("p (b t) -> p b t", b=GB)

                full = hT[:, batches(it, q), :]
                dve.wait_ge(one.tanh_ready, n)
                V.tensor_tensor(full, bt(go[:, q % 2, :]), bt(gg[:, q % 2, :]), ALU.mult).then_inc(one.h_full, 1)
                dve.wait_ge(one.h_full, n)
                V.tensor_copy(parts(h_hi), full).then_inc(one.h_hi, 1)
                dve.wait_ge(one.h_hi, n)
                V.tensor_tensor(parts(h_lo), full, parts(h_hi).bitcast(F32),
                                ALU.subtract).then_inc(one.h_ready.sem, 1)

            def graph_round(it, first):
                if not first:
                    one_step(it - 1, 0)
                for q in range(Q):
                    add_bias(it, q, bg0, xw_done, xw_ready)
                if first:
                    degree_roots(set_up)
                    scale_adjacency()
                else:
                    one_step(it - 1, 1)
                    one_step(it - 1, 2)
                for q in range(Q):
                    add_bias(it, q, bg1, hw_done, hw_ready)
                if not first:
                    one_step(it - 1, 3)
                for q in range(Q):
                    dve.wait_ge(g_hi_ready, it * Q + (q + 1))
                    V.scalar_tensor_tensor(out=g_lo[:, q, :], in0=bank[q][:, :], scalar=0.0,
                                           in1=g_hi[:, q, :].bitcast(F32), op0=ALU.max,
                                           op1=ALU.subtract).then_inc(g_lo_ready, 1)

            dve.wait_ge(first_in, 16)
            degrees(set_up)
            graph_round(0, True)
            with dve.Fori(1, ITERS) as it:
                graph_round(it, False)
            for q in range(Q):
                one_step(ITERS - 1, q)

            def window_step(p, it, j, s):
                w, n = win[p][s], WIN[p] * B
                c, i, f, g = (x[:, s, 0:n] for x in (cell, gi, gf, gg))
                read, h_ready = w.gate_read, w.h_ready

                def wait_gates(k):
                    dve.wait_ge(read.sem, read.at(it * gates_before(p), gates_before(j) + k))

                if j == 0:
                    wait_gates(2)
                    V.tensor_tensor(c, i, g, ALU.mult).then_inc(w.cell_ready, 1)
                else:
                    wait_gates(1)
                    V.tensor_tensor(c, f, c, ALU.mult).then_inc(w.term, 1)
                    wait_gates(3)
                    V.tensor_tensor(i, i, g, ALU.mult).then_inc(w.term, 1)
                    dve.wait_ge(w.term, it * (2 * (p - 1)) + 2 * j)
                    V.tensor_tensor(c, c, i, ALU.add).then_inc(w.cell_ready, 1)
                wait_gates(len(gates_of(p, j)))
                dve.wait_ge(w.tanh_ready, it * p + (j + 1))
                o_gate, tanh_c = tb(go[:, s, :], p), tb(gg[:, s, :], p)
                last = j == p - 1
                if last and p == 4:
                    full = tb(hbuf[:, s, :], p)
                    V.tensor_tensor(full, o_gate, tanh_c, ALU.mult).then_inc(w.h_full, 1)
                    dve.wait_ge(w.h_full, it * p + (j + 1))
                    dve.wait_ge(xres_in, 16)
                    x_at = windows_bt(x_res, p, it, s, j)
                    V.tensor_tensor(x_at, x_at, full, ALU.add).then_inc(h_ready.sem, 1)
                    return
                if last:
                    full = windows_bt(hT, p, it, s, j)
                    hi, lo = (windows(x, p, it, s, j) for x in (h_hi, h_lo))
                else:
                    full, hi, lo = (tb(x[:, s, :], p) for x in (hbuf, hs_hi, hs_lo))
                V.tensor_tensor(full, o_gate, tanh_c, ALU.mult).then_inc(w.h_full, 1)
                dve.wait_ge(w.h_full, it * p + (j + 1))
                V.tensor_copy(hi, full).then_inc(w.h_hi, 1)
                n_hi = it * p + (j + 1) if p < 4 else it * (p - 1) + (j + 1)
                dve.wait_ge(w.h_hi, n_hi)
                V.tensor_tensor(lo, full, hi.bitcast(F32), ALU.subtract).then_inc(h_ready.sem, 1)

            dve.wait_ge(lw_ready, 7)
            for p in WIN:
                for step in steps_of_pair(p, 0, (p - 1, PAIRS[p - 1] - 1, p - 2, 1) if p > 2 else None):
                    window_step(*step)
                with dve.Fori(1, PAIRS[p]) as it:
                    for step in steps_of_pair(p, it, (p, it - 1, p - 1, 1)):
                        window_step(*step)
            window_step(4, PAIRS[4] - 1, 3, 1)

            LN_STEPS = 5 + 5 + 1

            def ln_scalars(st, var_sem, sd_sem, count):
                me, qe, mo, qo = (lnst[:, :, k] for k in (1, 2, 4, 5))
                msum, dif, ssq, t, r, v, sd, nm = (lnsm[:, k, :] for k in range(8))
                st.settle()
                st.then(V.tensor_tensor(msum, me, mo, ALU.add))
                st.then(V.tensor_tensor(dif, me, mo, ALU.subtract))
                st.then(V.tensor_tensor(ssq, qe, qo, ALU.add))
                st.settle()
                st.then(V.tensor_tensor(dif, dif, dif, ALU.mult))
                st.then(V.tensor_scalar(ssq, ssq, 1.0 / P, EPS, ALU.mult, ALU.add))
                st.settle()
                V.scalar_tensor_tensor(out=v, in0=dif, scalar=0.25, in1=ssq, op0=ALU.mult,
                                       op1=ALU.add).then_inc(var_sem, 1)
                dve.wait_ge(sd_sem, count)
                newton(st, v, sd, r, t)
                st.then(V.scalar_tensor_tensor(out=nm, in0=msum, scalar=-0.5, in1=r, op0=ALU.mult,
                                               op1=ALU.mult))
                st.settle()

            def layer_norm(it, first):
                steps = Q * GB + LN_STEPS
                st = Steps(dve, ln_step, it * steps)
                for q in range(Q):
                    dve.wait_ge(res_t_done, it * Q + (q + 1))
                    for k in range(GB):
                        st.then(V.bn_stats(lnst[:, q * GB + k, :], bank[q][:, k * P:(k + 1) * P]))
                if not first:
                    dve.wait_ge(x1_act, it * 2)
                ln_scalars(st, ln_var, ln_sd, it + 1)
                assert st.n == steps
                for q in (0, 2):
                    if not first:
                        dve.wait_ge(agg_done, it * Q + (q + 1 - Q))
                        dve.wait_ge(x1_saved[q], it * 16)
                    for k in range(GB):
                        c = q * GB + k
                        last = V.tensor_scalar(x1s[:, q, k * P:(k + 1) * P], bank[q][:, k * P:(k + 1) * P],
                                               lnsm[:, 4, c:c + 1], lnsm[:, 7, c:c + 1], ALU.mult, ALU.add)
                        if q == 0 and k == 0:
                            last.then_inc(ln_ready, 1)
                        elif k == GB - 1:
                            last.then_inc(x1_dve, 1)

            def w1_stats(it):
                for q in range(Q):
                    for h in range(HC):
                        dve.wait_ge(w1_read.sem, w1_read.at(it * (HC * Q), HC * q + h + 1))
                        V.bn_stats(st1[:, h, bass.ds(it * Q + q, 1), :].rearrange("p a s -> p (a s)"),
                                   h1[:, h, grp(it * Q + q)]).then_inc(st1_done, 1)

            layer_norm(0, True)
            with dve.Fori(1, ITERS) as it:
                layer_norm(it, False)
                w1_stats(it - 1)
            w1_stats(ITERS - 1)

            bst = Steps(dve, bn_step)

            def bn_scalars(c0, n, g0, be0, count):
                v, sd, r, t = (bnsm[:, k, c0:c0 + n] for k in range(4))
                scale, shift = (bnsm[:, k, c0:c0 + n] for k in (6, 7))
                mean, var = mv[:, c0:c0 + n, 0], mv[:, c0:c0 + n, 1]
                bst.settle()
                V.tensor_scalar(v, var, EPS, None, ALU.add).then_inc(bn_var, 1)
                dve.wait_ge(bn_sd, count)
                newton(bst, v, sd, r, t)
                bst.then(V.tensor_tensor(scale, r, vecs[:, g0:g0 + n], ALU.mult))
                bst.settle()
                bst.then(V.tensor_tensor(t, mean, scale, ALU.mult))
                bst.settle()
                V.tensor_tensor(shift, vecs[:, be0:be0 + n], t, ALU.subtract).then_inc(bn_ready, 1)

            dve.wait_ge(st1_done, HC * G)
            for h in range(HC):
                bst.then(V.bn_aggr(mv[:, h, :], st1[:, h, :, :].rearrange("p a s -> p (a s)")))
            bn_scalars(0, HC, V_G1, V_BE1, 1)

            with dve.Fori(0, ITERS) as it:
                for q in range(Q):
                    dve.wait_ge(w2_done.sem, w2_done.at(it * Q, q + 1))
                    V.tensor_scalar(outT[:, grp(it * Q + q)], bank[q][:, :], vecs[:, V_B2:V_B2 + 1], None,
                                    ALU.add).then_inc(w2_read.sem, 1)
                    dve.wait_ge(w2_read.sem, w2_read.at(it * Q, q + 1))
                    V.bn_stats(st2[:, bass.ds(it * Q + q, 1), :].rearrange("p a s -> p (a s)"),
                               outT[:, grp(it * Q + q)]).then_inc(st2_done, 1)
            dve.wait_ge(st2_done, G)
            bst.then(V.bn_aggr(mv[:, 2, :], st2[:, :, :].rearrange("p a s -> p (a s)")))
            bn_scalars(2, 1, V_G2, V_BE2, 2)

            with dve.Fori(0, ITERS) as it:
                steps = Q * GB + LN_STEPS
                st = Steps(dve, ln2_step, it * steps)
                for q in range(Q):
                    dve.wait_ge(sT_t_done.sem, sT_t_done.at(it * Q, q + 1))
                    r2 = x1[:, batches(it, q), :]
                    V.tensor_tensor(r2, bank[4 + q][:, :].rearrange("p (b d) -> p b d", b=GB), r2,
                                    ALU.add).then_inc(r2_ready.sem, 1)
                    dve.wait_ge(r2_ready.sem, r2_ready.at(it * Q, q + 1))
                    for k in (1, 2, 3, 0):
                        b = x1[:, bass.ds(it * (Q * GB) + q * GB + k, 1), :].rearrange("p b d -> p (b d)")
                        st.then(V.bn_stats(lnst[:, q * GB + k, :], b))
                dve.wait_ge(out_act.sem, out_act.at(it * (Q - 1), 0))
                ln_scalars(st, ln2_var, ln2_sd, it + 1)
                assert st.n == steps
                q = Q - 1
                for k in range(GB):
                    c = q * GB + k
                    b = x1[:, bass.ds(it * (Q * GB) + c, 1), :].rearrange("p b d -> p (b d)")
                    last = V.tensor_scalar(b, b, lnsm[:, 4, c:c + 1], lnsm[:, 7, c:c + 1], ALU.mult, ALU.add)
                    if k == 0:
                        last.then_inc(ln2_ready, 1)
                    elif k == GB - 1:
                        last.then_inc(out_dve, 1)


def kernel(x, adj, L0_gnn_Wg0, L0_gnn_bg0, L0_gnn_Wg1, L0_gnn_bg1, L0_gnn_Wih, L0_gnn_Whh, L0_gnn_bih,
           L0_gnn_bhh, L1_gnn_W1, L1_gnn_b1, L1_gnn_g1, L1_gnn_be1, L1_gnn_W2, L1_gnn_b2, L1_gnn_g2,
           L1_gnn_be2):
    import numpy as np
    import concourse.bacc as bacc
    from concourse.bass_utils import run_bass_kernel_spmd

    a = np.asarray
    adj = a(adj)
    row = lambda v: np.broadcast_to(a(v)[None, :], (P, P))
    w2 = a(L1_gnn_W2).T.reshape(HC, P, P).transpose(1, 0, 2).reshape(P, HC * P)
    by_gate = lambda v: a(v).reshape(16, P).T
    chan = lambda v: a(v).reshape(-1, P).T
    wT = lambda w: a(w).transpose(2, 0, 1)
    arrays = {
        "xT": np.ascontiguousarray(a(x).transpose(2, 0, 1)),
        "mats": np.ascontiguousarray(np.concatenate(
            [a(L0_gnn_Wg0), row(L0_gnn_bg0), adj.T, adj, a(L0_gnn_Wg1), row(L0_gnn_bg1),
             a(L1_gnn_W1).T, w2], axis=1)),
        "lw": np.ascontiguousarray(np.concatenate([wT(L0_gnn_Wih), wT(L0_gnn_Whh)[:, 1:]], axis=1)),
        "vecs": np.ascontiguousarray(np.concatenate(
            [by_gate(L0_gnn_bih), by_gate(L0_gnn_bhh), chan(L1_gnn_b1), chan(L1_gnn_g1), chan(L1_gnn_be1),
             chan(L1_gnn_b2), chan(L1_gnn_g2), chan(L1_gnn_be2)], axis=1)),
    }
    nc = bacc.Bacc("TRN2", target_bir_lowering=False, num_devices=1)
    ins = [nc.dram_tensor(k + "_dram", v.shape, F32, kind="ExternalInput").ap() for k, v in arrays.items()]
    out = nc.dram_tensor("out_dram", (T, B, P), F32, kind="ExternalOutput").ap()
    build(nc, *ins, out)
    r = run_bass_kernel_spmd(nc, [{k + "_dram": v for k, v in arrays.items()}], core_ids=[0])
    return np.ascontiguousarray(r.results[0]["out_dram"].transpose(1, 0, 2))
```

```python
from contextlib import ExitStack

import concourse.bass as bass
from concourse import mybir

F32 = mybir.dt.float32
F32R = mybir.dt.float32r
ALU = mybir.AluOpType
ACT = mybir.ActivationFunctionType
AX = mybir.AxisListType

P = 128
B = 64
T = 128
GB = 4
NT = GB * T
G = B // GB
Q = 4
ITERS = G // Q
HC = 2
EPS = 1e-5
SIG_I, SIG_F, TANH_G, SIG_O = range(4)
FIRST_GATES = (SIG_I, TANH_G, SIG_O)
ALL_GATES = (SIG_F, SIG_I, TANH_G, SIG_O)
WIN = {2: 8, 3: 7, 4: 8}
PAIRS = {p: (T // p) // (2 * WIN[p]) for p in WIN}
for _p in WIN:
    assert PAIRS[_p] * 2 * WIN[_p] == T // _p
NMAT = 6
NFIRST = 4
V_BIH, V_BHH, V_B1, V_G1, V_BE1, V_B2, V_G2, V_BE2, V_END = 0, 16, 32, 34, 36, 38, 39, 40, 41


class Steps:

    def __init__(self, eng, sem, base=0):
        self.eng, self.sem, self.base, self.n = eng, sem, base, 0

    def then(self, ins):
        ins.then_inc(self.sem, 1)
        self.n += 1

    def settle(self):
        self.eng.wait_ge(self.sem, self.base + self.n)


class Flag:

    def __init__(self, sem, ahead=0):
        self.sem, self.ahead = sem, ahead

    def at(self, rounds, n):
        return rounds + (n + self.ahead)


def build(nc, xT_d, mats_d, lw_d, vecs_d, out_d):
    ctx = ExitStack()
    with ctx:
        base = nc.sbuf_base
        KB = 1024
        arena_bytes = 198 * KB
        ctx.enter_context(nc.sbuf_tensor("arena", [P, arena_bytes // 4], F32))
        start = base + (-base) % 32

        def at(name, off_kb, shape, dt=F32):
            size = 4
            for n in shape[1:]:
                size *= n
            assert off_kb * KB + size <= arena_bytes, name
            return nc.alloc_sbuf_tensor_at(name, shape, dt, offset=start + off_kb * KB)

        def sb(name, shape, dt=F32):
            return ctx.enter_context(nc.sbuf_tensor(name, shape, dt))

        hT = at("hT", 0, [P, B, T])
        h_hi = at("h_hi", 32, [P, T, B], F32R)
        h_lo = at("h_lo", 64, [P, T, B], F32R)
        xt_in = at("xt_in", 96, [P, Q, NT])
        ynat = at("ynat", 104, [P, Q, NT])
        h1T = at("h1T", 112, [P, Q, NT])
        g_hi = at("g_hi", 120, [P, Q, NT], F32R)
        g_lo = at("g_lo", 190, [P, Q, NT], F32R)
        lw_hi = at("lw_hi", 128, [P, 7, 512], F32R)
        lw_lo = at("lw_lo", 142, [P, 7, 512], F32R)
        gi = at("gi", 156, [P, 2, NT])
        gf = at("gf", 160, [P, 2, NT])
        gg = at("gg", 164, [P, 2, NT])
        go = at("go", 168, [P, 2, NT])
        cell = at("cell", 172, [P, 2, NT])
        anorm = at("anorm", 172, [P, P])
        lw_raw = at("lw_raw", 176, [P, 7, 512])
        hbuf = at("hbuf", 176, [P, 2, NT])
        hs_hi = at("hs_hi", 180, [P, 2, NT], F32R)
        hs_lo = at("hs_lo", 184, [P, 2, NT], F32R)
        x_res = at("x_res", 96, [P, B, T])
        h1 = at("h1", 32, [P, HC, G * NT])
        x1 = at("x1", 128, [P, B, P])
        res = at("res", 160, [P, Q, NT])
        x1s = at("x1s", 168, [P, Q, NT])
        aggT = at("aggT", 176, [P, Q, NT])
        hr = at("hr", 160, [P, Q, HC, NT])
        outT = at("outT", 0, [P, G * NT])

        mats = sb("mats", [P, NMAT * P + 2 * HC * P])
        vecs = sb("vecs", [P, V_END])
        wg0, bg0, adjT, adj, wg1, bg1 = (mats[:, k * P:(k + 1) * P] for k in range(NMAT))
        w1T = mats[:, NMAT * P:(NMAT + HC) * P].rearrange("p (h c) -> p h c", h=HC)
        w2T = mats[:, (NMAT + HC) * P:].rearrange("p (h c) -> p h c", h=HC)
        lbias = sb("lbias", [P, 4, 4])
        ident = sb("ident", [P, P])
        zeros = sb("zeros", [P, P])
        ahatT = sb("ahatT", [P, P])
        dsm = sb("dsm", [P, 8])
        lnst = sb("lnst", [P, 2, Q * GB, 6])
        lnsm = sb("lnsm", [P, 2, 8, Q * GB])
        st1 = sb("st1", [P, HC, G, 6])
        st2 = sb("st2", [P, G, 6])
        mv = sb("mv", [P, 3, 2])
        bnsm = sb("bnsm", [P, 8, 3])
        bank = [ctx.enter_context(nc.psum_tensor(f"bank{i}", [P, NT], F32)) for i in range(8)]

        def sem(name):
            return ctx.enter_context(nc.semaphore(name))

        first_in, mats_in, vecs_in, lw_in = sem("first_in"), sem("mats_in"), sem("vecs_in"), sem("lw_in")
        x_in = [sem(f"x_in{q}") for q in range(Q)]
        zeros_ready = sem("zeros_ready")
        ident_step, lw_hi_ready, lw_ready = sem("ident_step"), sem("lw_hi_ready"), sem("lw_ready")
        dve_set, lbias_ready = sem("dve_set"), sem("lbias_ready")
        deg_ready, deg_root, dinv_ready = sem("deg_ready"), sem("deg_root"), sem("dinv_ready")
        drow_ready, ahat_ready = sem("drow_ready"), sem("ahat_ready")
        xw_done, xw_ready = sem("xw_done"), sem("xw_ready")
        ag1_done, h1_ready = sem("ag1_done"), sem("h1_ready")
        hw_done, hw_ready = sem("hw_done"), sem("hw_ready")
        ag2_done, g_hi_ready, g_lo_ready = sem("ag2_done"), sem("g_hi_ready"), sem("g_lo_ready")

        class CellFlags:
            def __init__(self, name, banks, slots):
                self.gate_done = sem(f"{name}_gate_done")
                self.gate_read = Flag(sem(f"{name}_gate_read"), banks)
                self.term = sem(f"{name}_term")
                self.cell_ready = sem(f"{name}_cell")
                self.tanh_ready = sem(f"{name}_tanh")
                self.h_full = sem(f"{name}_h_full")
                self.h_hi = sem(f"{name}_h_hi")
                self.h_ready = Flag(sem(f"{name}_h_ready"), slots)

        one = CellFlags("p1", 4, 2)
        win = {p: [CellFlags(f"p{p}s{s}", 1, 1) for s in range(2)] for p in WIN}
        xres_in, early_sum = sem("xres_in"), sem("early_sum")
        res_in = [sem(f"res_in{q}") for q in range(Q)]
        res_t_done = sem("res_t_done")
        ln_step, ln_var, ln_sd, ln_ready = sem("ln_step"), sem("ln_var"), sem("ln_sd"), sem("ln_ready")
        x1_dve, x1_act = sem("x1_dve"), sem("x1_act")
        x1_saved = [sem(f"x1_saved{q}") for q in range(Q)]
        agg_done, agg_ready = sem("agg_done"), sem("agg_ready")
        w1_done, w1_read, st1_done = sem("w1_done"), Flag(sem("w1_read"), 2 * HC), sem("st1_done")
        bn_step, bn_var, bn_sd, bn_ready = sem("bn_step"), sem("bn_var"), sem("bn_sd"), sem("bn_ready")
        hr_ready, w2_done = sem("hr_ready"), Flag(sem("w2_done"), Q)
        w2_read, st2_done = Flag(sem("w2_read"), Q), sem("st2_done")
        bn2_done, sum_done = sem("bn2_done"), sem("sum_done")
        ln2_step, ln2_var, ln2_sd, ln2_ready = sem("ln2_step"), sem("ln2_var"), sem("ln2_sd"), sem("ln2_ready")
        out_act, out_dve, out_saved = sem("out_act"), sem("out_dve"), sem("out_saved")

        ihw = lambda p: p - 1
        hhw = lambda p: 4 + p - 2
        gates_of = lambda p, j: FIRST_GATES if j == 0 else ALL_GATES
        gates_before = lambda j: 0 if j == 0 else 3 + 4 * (j - 1)
        gcols = lambda g: slice(g * P, (g + 1) * P)

        def grp(n):
            return bass.ds(n * NT, NT)

        def batches(it, q):
            return bass.ds(it * (Q * GB) + q * GB, GB)

        def w1_bank(q, h):
            return bank[(4 if q in (0, 3) else 6) + h]

        def sum_bank(r, q):
            return bank[(4 if r % 2 == 0 else 0) + q]

        act_groups = lambda r: range(Q - 1 if r < ITERS - 1 else Q // 2)
        dve_groups = lambda r: range(act_groups(r).stop, Q)

        def normalised(r, q):
            if q in act_groups(r):
                return out_act, sum(len(act_groups(i)) for i in range(r)) + q + 1
            return out_dve, sum(len(dve_groups(i)) for i in range(r)) + q - dve_groups(r).start + 1

        def tile_start(p, it, s):
            return it * (2 * WIN[p] * p) + s * WIN[p] * p

        def windows(buf, p, it, s, j):
            return buf[:, bass.ds(tile_start(p, it, s), p * WIN[p]), :].rearrange(
                "p (w j) b -> p w j b", j=p)[:, :, j, :]

        def windows_bt(buf, p, it, s, j):
            return buf[:, :, bass.ds(tile_start(p, it, s), p * WIN[p])].rearrange(
                "p b (w j) -> p w j b", j=p)[:, :, j, :]

        def tb(ap, p):
            return ap[:, 0:WIN[p] * B].rearrange("p (w b) -> p w b", b=B)

        def steps_of_pair(p, it, before):
            for j in range(p):
                yield p, it, j, 0
                if j:
                    yield p, it, j - 1, 1
                elif before:
                    yield before

        def sums_ready(eng):
            eng.wait_ge(early_sum, 8)
            for w in win[4]:
                eng.wait_ge(w.h_ready.sem, w.h_ready.at(0, 4 * PAIRS[4]))

        block = ctx.enter_context(nc.Block())

        @block.sync
        def _(sp):
            sp.dma_start(mats[:, 0:NFIRST * P], mats_d[:, 0:NFIRST * P]).then_inc(first_in, 16)

            def load(it, q):
                sp.dma_start(xt_in[:, q, :].rearrange("p (b s) -> p b s", b=GB),
                             xT_d[:, batches(it, q), :]).then_inc(x_in[q], 16)

            for q in range(1, Q):
                load(0, q)
            sp.dma_start(mats[:, NFIRST * P:], mats_d[:, NFIRST * P:]).then_inc(mats_in, 16)
            sp.dma_start(vecs[:, :], vecs_d).then_inc(vecs_in, 16)
            sp.dma_start(lw_raw[:, :, :], lw_d).then_inc(lw_in, 16)
            with sp.Fori(1, ITERS) as it:
                for q in range(Q):
                    sp.wait_ge(xw_done, it * Q + (q + 1 - Q))
                    load(it, q)
            sp.wait_ge(one.gate_done, 3 * G)
            sp.dma_start(x_res[:, :, :], xT_d).then_inc(xres_in, 16)

            def stage(it, q):
                sp.dma_start(res[:, q, :].rearrange("p (b t) -> p b t", b=GB),
                             x_res[:, batches(it, q), :]).then_inc(res_in[q], 16)

            def save(it, q):
                sp.wait_ge(x1_act if q else x1_dve, it * (Q - 1) + q if q else it + 1)
                sp.dma_start(x1[:, batches(it, q), :],
                             x1s[:, q, :].rearrange("p (b d) -> p b d", b=GB)).then_inc(x1_saved[q], 16)

            sums_ready(sp)
            for q in range(Q):
                stage(1, q)
            for q in range(Q):
                save(0, q)
            with sp.Fori(2, ITERS) as it:
                for q in range(Q):
                    sp.wait_ge(res_t_done, it * Q + (q + 1 - Q))
                    stage(it, q)
                for q in range(Q):
                    save(it - 1, q)
            for q in range(Q):
                save(ITERS - 1, q)

            for r in range(ITERS):
                for q in (0, 3, 1, 2) if r < ITERS - 1 else (0, 2, 1, 3):
                    sp.wait_ge(*normalised(r, q))
                    own = slice((r * Q + q) * GB, (r * Q + q + 1) * GB)
                    sp.dma_start(out_d[:, own, :], x1[:, own, :]).then_inc(out_saved, 16)
            sp.wait_ge(out_saved, 16 * G)

        @block.gpsimd
        def _(pool):
            nc.gpsimd.memset(ident[:, :], 0.0).then_inc(ident_step, 1)
            pool.wait_ge(ident_step, 1)
            nc.gpsimd.affine_select(out=ident[:, :], in_=ident[:, :], compare_op=ALU.not_equal, fill=1.0,
                                    base=0, pattern=[[-1, P]], channel_multiplier=1).then_inc(ident_step, 1)
            pool.wait_ge(lw_in, 16)
            for k in range(7):
                nc.gpsimd.tensor_copy(lw_hi[:, k, :], lw_raw[:, k, :]).then_inc(lw_hi_ready, 1)
                pool.wait_ge(lw_hi_ready, k + 1)
                nc.gpsimd.tensor_tensor(lw_lo[:, k, :], lw_raw[:, k, :], lw_hi[:, k, :].bitcast(F32),
                                        ALU.subtract).then_inc(lw_ready, 1)
            pool.wait_ge(xres_in, 16)
            for s in range(2):
                f = win[3][s].h_ready
                pool.wait_ge(f.sem, f.at(0, 3 * PAIRS[3]))
            with pool.Fori(0, 8) as it:
                def early(buf):
                    return buf[:, bass.ds(it * 8, 8), :].rearrange("p b (w j) -> p b w j", j=4)[:, :, :, 0:3]

                nc.gpsimd.tensor_tensor(early(x_res), early(x_res), early(hT), ALU.add).then_inc(early_sum, 1)

        @block.tensor
        def _(pe):
            pe.sem_inc(w2_done.sem, w2_done.ahead)

            def keep_warm(free_bank, products):
                for _ in range(products):
                    nc.tensor.matmul(free_bank[:, 0:P], zeros[:, :], zeros[:, :], start=True, stop=True)

            def split_products(out, wk, gate, hi, lo, start, stop, lo_ready=None):
                cols = gcols(gate)
                nc.tensor.matmul(out, lw_lo[:, wk, cols], hi, start=start, stop=False)
                nc.tensor.matmul(out, lw_hi[:, wk, cols], hi, start=False, stop=False)
                if lo_ready:
                    pe.wait_ge(*lo_ready)
                return nc.tensor.matmul(out, lw_hi[:, wk, cols], lo, start=False, stop=stop)

            def data_stationary(q, data, moving, done):
                for k in range(GB):
                    last = nc.tensor.matmul(bank[q][:, k * P:(k + 1) * P], data[:, q, k * P:(k + 1) * P],
                                            moving, start=True, stop=True)
                last.then_inc(done, 1)

            def one_step(it, q):
                pe.wait_ge(g_lo_ready, it * Q + (q + 1))
                for k, gate in enumerate(FIRST_GATES):
                    m = 3 * q + k
                    pe.wait_ge(one.gate_read.sem, one.gate_read.at(it * (3 * Q), m - 3))
                    split_products(bank[4 + m % 4][:, :], ihw(1), gate, g_hi[:, q, :], g_lo[:, q, :],
                                   True, True).then_inc(one.gate_done, 1)

            def graph_round(it, first):
                for q in range(Q):
                    pe.wait_ge(x_in[q], it * 16 + 16)
                    if not first:
                        pe.wait_ge(g_lo_ready, it * Q + (q + 1 - Q))
                    data_stationary(q, xt_in, wg0, xw_done)
                if not first:
                    one_step(it - 1, 2)
                for q in range(Q):
                    pe.wait_ge(xw_ready, it * Q + (q + 1))
                    data_stationary(q, ynat, adjT, ag1_done)
                if first:
                    pe.wait_ge(ident_step, 2)
                    pe.wait_ge(dinv_ready, 1)
                    nc.tensor.matmul(bank[4][:, 0:P], anorm[:, :], ident[:, :],
                                     start=True, stop=True).then_inc(drow_ready, 1)
                    pe.wait_ge(mats_in, 16)
                else:
                    one_step(it - 1, 3)
                for q in range(Q):
                    pe.wait_ge(h1_ready, it * Q + (q + 1))
                    data_stationary(q, h1T, wg1, hw_done)
                for q in range(Q):
                    pe.wait_ge(hw_ready, it * Q + (q + 1))
                    data_stationary(q, ynat, adjT, ag2_done)
                    if q == Q - 2:
                        if first:
                            pe.wait_ge(ahat_ready, 1)
                            pe.wait_ge(lw_ready, 1)
                        one_step(it, 0)
                one_step(it, 1)

            pe.wait_ge(zeros_ready, 1)
            keep_warm(bank[4], 7)
            pe.wait_ge(first_in, 16)
            graph_round(0, True)
            with pe.Fori(1, ITERS) as it:
                graph_round(it, False)
            one_step(ITERS - 1, 2)
            one_step(ITERS - 1, 3)
            pe.wait_ge(lw_ready, 7)
            pe.wait_ge(g_lo_ready, G)
            keep_warm(bank[0], 24)

            pe.wait_ge(one.h_ready.sem, one.h_ready.at(0, G))
            pe.wait_ge(one.gate_read.sem, one.gate_read.at(0, 3 * G))

            def window_step(p, it, j, s):
                w = win[p][s]
                if p > 2 and j == 0:
                    for i in range(PAIRS[p]):
                        need = -(-2 * WIN[p] * p * (i + 1) // (2 * WIN[p - 1] * (p - 1)))
                        assert min(need, PAIRS[p - 1]) <= i + 2 <= PAIRS[p - 1]
                    for f in (win[p - 1][0].h_ready, win[p - 1][1].h_ready):
                        pe.wait_ge(f.sem, f.at(it * (p - 1), 2 * (p - 1)))
                    if isinstance(it, int):
                        f = win[p - 1][s].gate_read
                        pe.wait_ge(f.sem, f.at(0, gates_before(p - 1) * PAIRS[p - 1]))
                hi, lo = (windows(x, p, it, s, j) for x in (h_hi, h_lo))
                pe.wait_ge(w.gate_read.sem, w.gate_read.at(it * gates_before(p), gates_before(j)))
                for k, gate in enumerate(gates_of(p, j)):
                    last = split_products(tb(bank[4 * s + k], p), ihw(p), gate, hi, lo, True, j == 0)
                    if j == 0:
                        last.then_inc(w.gate_done, 1)
                if j:
                    pe.wait_ge(w.h_hi, it * min(p, 3) + j)
                    lo_ready = w.h_ready.sem, w.h_ready.at(it * p, j)
                    for k, gate in enumerate(ALL_GATES):
                        split_products(tb(bank[4 * s + k], p), hhw(p), gate, tb(hs_hi[:, s, :], p),
                                       tb(hs_lo[:, s, :], p), False, True,
                                       None if k else lo_ready).then_inc(w.gate_done, 1)

            for p in WIN:
                for step in steps_of_pair(p, 0, (p - 1, PAIRS[p - 1] - 1, p - 2, 1) if p > 2 else None):
                    window_step(*step)
                with pe.Fori(1, PAIRS[p]) as it:
                    for step in steps_of_pair(p, it, (p, it - 1, p - 1, 1)):
                        window_step(*step)
            window_step(4, PAIRS[4] - 1, 3, 1)

            for s in range(2):
                f = win[4][s].gate_read
                pe.wait_ge(f.sem, f.at(0, gates_before(4) * PAIRS[4]))
                if s == 0:
                    keep_warm(bank[0], 12)

            def to_nat(it, q, first=False):
                if not first:
                    pe.wait_ge(res_in[q], it * 16)
                for k in range(GB):
                    last = nc.tensor.transpose(bank[q][:, k * P:(k + 1) * P],
                                               x_res[:, q * GB + k, :] if first else
                                               res[:, q, k * P:(k + 1) * P], ident[:, :])
                last.then_inc(res_t_done, 1)

            def aggregate(it, q):
                pe.wait_ge(x1_act if q else x1_dve, it * (Q - 1) + q if q else it + 1)
                if not (isinstance(it, int) and it == 0):
                    pe.wait_ge(w1_read.sem, w1_read.at(it * (HC * Q), HC * (q // 2 * 2 - Q) + q % 2 + 1))
                for k in range(GB):
                    last = nc.tensor.matmul(bank[4 + q][:, k * P:(k + 1) * P], x1s[:, q, k * P:(k + 1) * P],
                                            ahatT[:, :], start=True, stop=True)
                last.then_inc(agg_done, 1)

            def first_product(it, q, alone=False):
                if q < 2:
                    pe.wait_ge(agg_ready, it * Q + (Q if q else 1))
                elif q == 3 and not alone:
                    pe.wait_ge(agg_ready, it * Q + (Q + 2))
                for h in range(HC):
                    if q in (0, 2) or alone:
                        before = 0 if q == 3 else q - 1
                        pe.wait_ge(w1_read.sem, w1_read.at(it * (HC * Q), HC * before + h + 1))
                    nc.tensor.matmul(w1_bank(q, h)[:, :], w1T[:, h, :], aggT[:, q, :],
                                     start=True, stop=True).then_inc(w1_done, 1)

            def norm_round(it, back, ahead):
                def nat(q):
                    if ahead:
                        pe.wait_ge(x1_act if q else x1_dve, it * (Q - 1) + q if q else it + 1)
                        to_nat(it + 1, q)

                for q in range(2):
                    nat(q)
                    aggregate(it, q)
                if back:
                    first_product(it - 1, 2)
                    first_product(it - 1, 3)
                nat(2)
                nat(3)
                aggregate(it, 2)
                aggregate(it, 3)
                first_product(it, 0)
                first_product(it, 1)

            sums_ready(pe)
            for q in range(Q):
                to_nat(0, q, True)
            keep_warm(bank[4], 20)
            norm_round(0, False, True)
            with pe.Fori(1, ITERS - 1) as it:
                norm_round(it, True, True)
            norm_round(ITERS - 1, True, False)
            first_product(ITERS - 1, 2, True)
            first_product(ITERS - 1, 3, True)

            def add_x1(r, q):
                g = r * Q + q
                nc.tensor.matmul(sum_bank(r, q)[:, :], ident[:, :],
                                 x1[:, g * GB:(g + 1) * GB, :].rearrange("p b d -> p (b d)"),
                                 start=True, stop=False)

            for q in range(Q):
                pe.wait_ge(x1_saved[q], 16 * ITERS)
            pe.wait_ge(w1_read.sem, w1_read.at(0, HC * G))
            for q in range(Q):
                add_x1(0, q)
            keep_warm(bank[0], 2)

            with pe.Fori(0, ITERS) as it:
                for q in range(Q):
                    pe.wait_ge(w2_read.sem, w2_read.at(it * Q, q + 1 - Q))
                    for h in range(HC):
                        pe.wait_ge(hr_ready, it * (HC * Q) + (HC * q + h + 1))
                        last = nc.tensor.matmul(bank[q][:, :], w2T[:, h, :], hr[:, q, h, :],
                                                start=h == 0, stop=h == HC - 1)
                    last.then_inc(w2_done.sem, 1)

            for q in range(Q):
                pe.wait_ge(w2_read.sem, w2_read.at(0, G - Q + q + 1))
                add_x1(1, q)
            for r in range(ITERS):
                for q in range(Q):
                    pe.wait_ge(bn2_done, r * Q + q + 1)
                    for k in range(GB):
                        last = nc.tensor.matmul(sum_bank(r, q)[:, k * P:(k + 1) * P],
                                                outT[:, (r * Q + q) * NT + k * P:(r * Q + q) * NT + (k + 1) * P],
                                                ident[:, :], start=False, stop=k == GB - 1)
                    last.then_inc(sum_done, 1)
                if 1 <= r < ITERS - 1:
                    for q in range(Q):
                        pe.wait_ge(*normalised(r - 1, q))
                        add_x1(r + 1, q)

        @block.scalar
        def _(act):
            act.dma_start(xt_in[:, 0, :].rearrange("p (b s) -> p b s", b=GB), xT_d[:, 0:GB, :]).then_inc(x_in[0], 16)
            for f in [one.gate_read, w1_read] + [w.gate_read for p in WIN for w in win[p]]:
                act.sem_inc(f.sem, f.ahead)
            act.wait_ge(deg_ready, 1)
            nc.scalar.activation(dsm[:, 4:5], dsm[:, 3:4], ACT.Sqrt).then_inc(deg_root, 1)

            def gate(out, src, p, g, done):
                nc.scalar.activation(out, src, ACT.Tanh if g == TANH_G else ACT.Sigmoid,
                                     bias=lbias[:, p - 1, g:g + 1]).then_inc(done.sem, 1)

            gbuf = {SIG_I: gi, SIG_F: gf, TANH_G: gg, SIG_O: go}

            def one_gates(it, q):
                if not (isinstance(it, int) and it * Q + q < 2):
                    act.wait_ge(one.h_full, it * Q + (q - 1))
                for k, g in enumerate(FIRST_GATES):
                    m = 3 * q + k
                    act.wait_ge(one.gate_done, it * (3 * Q) + (m + 1))
                    gate(gbuf[g][:, q % 2, :], bank[4 + m % 4][:, :], 1, g, one.gate_read)

            def one_tanh(it, q):
                act.wait_ge(one.cell_ready, it * Q + (q + 1))
                nc.scalar.activation(gg[:, q % 2, :], cell[:, q % 2, :], ACT.Tanh).then_inc(one.tanh_ready, 1)

            def graph_round(it, first):
                if not first:
                    one_gates(it - 1, 2)
                    one_tanh(it - 1, 2)
                for q in range(Q):
                    act.wait_ge(ag1_done, it * Q + (q + 1))
                    nc.scalar.activation(h1T[:, q, :], bank[q][:, :], ACT.Relu).then_inc(h1_ready, 1)
                if not first:
                    one_gates(it - 1, 3)
                    one_tanh(it - 1, 3)
                for q in range(Q):
                    if q == Q - 1:
                        if first:
                            act.wait_ge(lbias_ready, 1)
                        one_gates(it, 0)
                    act.wait_ge(ag2_done, it * Q + (q + 1))
                    nc.scalar.activation(g_hi[:, q, :], bank[q][:, :], ACT.Relu).then_inc(g_hi_ready, 1)
                one_tanh(it, 0)
                one_gates(it, 1)
                one_tanh(it, 1)

            graph_round(0, True)
            with act.Fori(1, ITERS) as it:
                graph_round(it, False)
            for q in (2, 3):
                one_gates(ITERS - 1, q)
                one_tanh(ITERS - 1, q)

            def window_step(p, it, j, s):
                w, n = win[p][s], WIN[p] * B
                if j == 0:
                    if not isinstance(it, int):
                        act.wait_ge(w.h_full, it * p)
                    elif p > 2:
                        act.wait_ge(win[p - 1][s].h_full, (p - 1) * PAIRS[p - 1])
                for k, g in enumerate(gates_of(p, j)):
                    act.wait_ge(w.gate_done, it * gates_before(p) + (gates_before(j) + k + 1))
                    gate(gbuf[g][:, s, 0:n], bank[4 * s + k][:, 0:n], p, g, w.gate_read)
                act.wait_ge(w.cell_ready, it * p + (j + 1))
                nc.scalar.activation(gg[:, s, 0:n], cell[:, s, 0:n], ACT.Tanh).then_inc(w.tanh_ready, 1)

            act.wait_ge(one.h_full, G)
            for p in WIN:
                for step in steps_of_pair(p, 0, (p - 1, PAIRS[p - 1] - 1, p - 2, 1) if p > 2 else None):
                    window_step(*step)
                with act.Fori(1, PAIRS[p]) as it:
                    for step in steps_of_pair(p, it, (p, it - 1, p - 1, 1)):
                        window_step(*step)
            window_step(4, PAIRS[4] - 1, 3, 1)

            def agg_out(it, q):
                act.wait_ge(agg_done, it * Q + (q + 1))
                nc.scalar.activation(aggT[:, q, :], bank[4 + q][:, :], ACT.Copy).then_inc(agg_ready, 1)

            def w1_out(it, q):
                for h in range(HC):
                    act.wait_ge(w1_done, it * (HC * Q) + (HC * q + h + 1))
                    nc.scalar.activation(h1[:, h, grp(it * Q + q)], w1_bank(q, h)[:, :], ACT.Identity,
                                         bias=vecs[:, V_B1 + h:V_B1 + h + 1]).then_inc(w1_read.sem, 1)

            def ln_root(it, var, sd, half=0):
                act.wait_ge(var, it + 1)
                nc.scalar.activation(lnsm[:, half, 6, :], lnsm[:, half, 5, :], ACT.Sqrt).then_inc(sd, 1)

            def normalise(it, q, first):
                act.wait_ge(ln_ready, it + 1)
                if not first:
                    act.wait_ge(agg_done, it * Q + (q + 1 - Q))
                    act.wait_ge(x1_saved[q], it * 16)
                for k in range(GB):
                    c = q * GB + k
                    last = nc.scalar.activation(
                        x1s[:, q, k * P:(k + 1) * P], bank[q][:, k * P:(k + 1) * P], ACT.Identity,
                        bias=lnsm[:, 0, 7, c:c + 1], scale=lnsm[:, 0, 4, c:c + 1])
                last.then_inc(x1_act, 1)

            def norm_round(it, first, ahead):
                agg_out(it, 0)
                if not first:
                    normalise(it, 2, False)
                agg_out(it, 1)
                if not first:
                    w1_out(it - 1, 2)
                normalise(it, 3, first)
                if not first:
                    w1_out(it - 1, 3)
                agg_out(it, 2)
                agg_out(it, 3)
                if ahead:
                    ln_root(it + 1, ln_var, ln_sd)
                w1_out(it, 0)
                if ahead:
                    normalise(it + 1, 1, False)
                w1_out(it, 1)

            ln_root(0, ln_var, ln_sd)
            normalise(0, 1, True)
            normalise(0, 2, True)
            norm_round(0, True, True)
            with act.Fori(1, ITERS - 1) as it:
                norm_round(it, False, True)
            norm_round(ITERS - 1, False, False)
            for q in (2, 3):
                w1_out(ITERS - 1, q)

            act.wait_ge(bn_var, 1)
            nc.scalar.activation(bnsm[:, 1, 0:HC], bnsm[:, 0, 0:HC], ACT.Sqrt).then_inc(bn_sd, 1)
            act.wait_ge(bn_ready, 1)
            for q in range(Q):
                act.wait_ge(x1_saved[q], 16 * ITERS)
            with act.Fori(0, ITERS) as it:
                for q in range(Q):
                    act.wait_ge(w2_done.sem, w2_done.at(it * Q, q + 1 - Q))
                    for h in range(HC):
                        nc.scalar.activation(hr[:, q, h, :], h1[:, h, grp(it * Q + q)], ACT.Relu,
                                             bias=bnsm[:, 7, h:h + 1], scale=bnsm[:, 6, h:h + 1]
                                             ).then_inc(hr_ready, 1)

            act.wait_ge(bn_var, 2)
            nc.scalar.activation(bnsm[:, 1, 2:3], bnsm[:, 0, 2:3], ACT.Sqrt).then_inc(bn_sd, 1)
            act.wait_ge(bn_ready, 2)

            def bn2(g):
                own = outT[:, g * NT:(g + 1) * NT]
                nc.scalar.activation(own, own, ACT.Identity, bias=bnsm[:, 7, 2:3],
                                     scale=bnsm[:, 6, 2:3]).then_inc(bn2_done, 1)

            for g in range(2 * Q):
                bn2(g)
            for r in range(ITERS):
                ln_root(r, ln2_var, ln2_sd, r % 2)
                ahead = [(r + 2) * Q + q for q in range(Q if r + 2 < ITERS else 0)]
                for g in ([(r + 2) * Q - 1] if 0 < r < ITERS - 1 else []) + ahead[:2]:
                    bn2(g)
                act.wait_ge(ln2_ready, r + 1)
                for q in act_groups(r):
                    for k in range(GB):
                        c = q * GB + k
                        last = nc.scalar.activation(
                            x1[:, r * Q * GB + c, :], sum_bank(r, q)[:, k * P:(k + 1) * P], ACT.Identity,
                            bias=lnsm[:, r % 2, 7, c:c + 1], scale=lnsm[:, r % 2, 4, c:c + 1])
                    last.then_inc(out_act, 1)
                for g in ahead[2:3]:
                    bn2(g)

        @block.vector
        def _(dve):
            V = nc.vector
            V.memset(zeros[:, :], 0.0).then_inc(zeros_ready, 1)
            for f in [one.h_ready, w2_read] + [w.h_ready for p in WIN for w in win[p]]:
                dve.sem_inc(f.sem, f.ahead)

            def newton(st, v, sd, r, t):
                st.then(V.reciprocal(r, sd))
                st.settle()
                st.then(V.scalar_tensor_tensor(out=t, in0=r, scalar=-0.5, in1=r, op0=ALU.mult, op1=ALU.mult))
                st.settle()
                st.then(V.tensor_tensor(t, t, v, ALU.mult))
                st.settle()
                st.then(V.scalar_tensor_tensor(out=r, in0=t, scalar=1.5, in1=r, op0=ALU.add, op1=ALU.mult))
                st.settle()

            set_up = Steps(dve, dve_set)

            def degrees(st):
                dve.wait_ge(ident_step, 2)
                st.then(V.tensor_tensor(anorm[:, :], adj, ident[:, :], ALU.add))
                st.then(V.tensor_tensor(ahatT[:, :], adjT, ident[:, :], ALU.add))
                st.settle()
                st.then(V.reduce_sum(dsm[:, 0:1], anorm[:, :], AX.X))
                st.then(V.reduce_sum(dsm[:, 1:2], ahatT[:, :], AX.X))
                st.settle()
                st.then(V.tensor_tensor(anorm[:, :], anorm[:, :], ident[:, :], ALU.mult))
                st.settle()
                st.then(V.reduce_sum(dsm[:, 2:3], anorm[:, :], AX.X))
                st.then(V.tensor_tensor(dsm[:, 1:2], dsm[:, 0:1], dsm[:, 1:2], ALU.add))
                st.settle()
                V.tensor_tensor(dsm[:, 3:4], dsm[:, 1:2], dsm[:, 2:3], ALU.subtract).then_inc(deg_ready, 1)

            def degree_roots(st):
                dve.wait_ge(deg_root, 1)
                newton(st, dsm[:, 3:4], dsm[:, 4:5], dsm[:, 5:6], dsm[:, 6:7])
                st.then(V.memset(anorm[:, :], 0.0))
                st.settle()
                V.tensor_scalar(anorm[:, :], anorm[:, :], dsm[:, 5:6], None, ALU.add).then_inc(dinv_ready, 1)

            def scale_adjacency():
                dve.wait_ge(drow_ready, 1)
                V.scalar_tensor_tensor(out=ahatT[:, :], in0=ahatT[:, :], scalar=dsm[:, 5:6],
                                       in1=bank[4][:, 0:P], op0=ALU.mult, op1=ALU.mult).then_inc(ahat_ready, 1)
                dve.wait_ge(vecs_in, 16)
                V.tensor_tensor(lbias[:, :, :].rearrange("p a b -> p (a b)"), vecs[:, V_BIH:V_BHH],
                                vecs[:, V_BHH:V_B1], ALU.add).then_inc(lbias_ready, 1)

            def add_bias(it, q, b, done, ready):
                dve.wait_ge(done, it * Q + (q + 1))
                V.tensor_tensor(ynat[:, q, :].rearrange("p (k c) -> p k c", k=GB),
                                bank[q][:, :].rearrange("p (k c) -> p k c", k=GB),
                                b[:, None, :].to_broadcast([P, GB, P]), ALU.add).then_inc(ready, 1)

            def one_cell(it, q):
                dve.wait_ge(one.gate_read.sem, one.gate_read.at(it * (3 * Q), 3 * (q + 1)))
                V.tensor_tensor(cell[:, q % 2, :], gi[:, q % 2, :], gg[:, q % 2, :],
                                ALU.mult).then_inc(one.cell_ready, 1)

            def one_parts_at(buf, it, q):
                return buf[:, :, batches(it, q)].rearrange("p t b -> p b t")

            def one_full(it, q):
                o_gate, tanh_c = (x[:, q % 2, :].rearrange("p (b t) -> p b t", b=GB) for x in (go, gg))
                dve.wait_ge(one.tanh_ready, it * Q + (q + 1))
                V.tensor_tensor(hT[:, batches(it, q), :], o_gate, tanh_c, ALU.mult).then_inc(one.h_full, 1)

            def one_hi(it, q):
                dve.wait_ge(one.h_full, it * Q + (q + 1))
                V.tensor_copy(one_parts_at(h_hi, it, q), hT[:, batches(it, q), :]).then_inc(one.h_hi, 1)

            def one_lo(it, q):
                dve.wait_ge(one.h_hi, it * Q + (q + 1))
                V.tensor_tensor(one_parts_at(h_lo, it, q), hT[:, batches(it, q), :],
                                one_parts_at(h_hi, it, q).bitcast(F32), ALU.subtract
                                ).then_inc(one.h_ready.sem, 1)

            def relu_lo(it, q):
                dve.wait_ge(g_hi_ready, it * Q + (q + 1))
                V.scalar_tensor_tensor(out=g_lo[:, q, :], in0=bank[q][:, :], scalar=0.0,
                                       in1=g_hi[:, q, :].bitcast(F32), op0=ALU.max,
                                       op1=ALU.subtract).then_inc(g_lo_ready, 1)

            def in_turn(it, q, others):
                for step in (one_cell, one_full, one_hi, one_lo):
                    step(it, q)
                    if others:
                        others.pop(0)()
                for other in others:
                    other()

            def graph_round(it, first):
                xw = [lambda q=q: add_bias(it, q, bg0, xw_done, xw_ready) for q in range(Q)]
                hw = [lambda q=q: add_bias(it, q, bg1, hw_done, hw_ready) for q in range(Q)]
                if first:
                    for other in xw:
                        other()
                    degree_roots(set_up)
                    scale_adjacency()
                    for other in hw:
                        other()
                else:
                    in_turn(it - 1, 1, xw)
                    in_turn(it - 1, 2, [])
                    in_turn(it - 1, 3, hw)
                for q in range(Q - 1):
                    relu_lo(it, q)
                in_turn(it, 0, [lambda: relu_lo(it, Q - 1)])

            dve.wait_ge(first_in, 16)
            degrees(set_up)
            graph_round(0, True)
            with dve.Fori(1, ITERS) as it:
                graph_round(it, False)
            for q in range(1, Q):
                in_turn(ITERS - 1, q, [])

            def step_cell(p, it, j, s):
                w, n = win[p][s], WIN[p] * B
                c, i, f, g = (x[:, s, 0:n] for x in (cell, gi, gf, gg))
                read = w.gate_read

                def wait_gates(k):
                    dve.wait_ge(read.sem, read.at(it * gates_before(p), gates_before(j) + k))

                if j == 0:
                    wait_gates(2)
                    V.tensor_tensor(c, i, g, ALU.mult).then_inc(w.cell_ready, 1)
                else:
                    wait_gates(1)
                    V.tensor_tensor(c, f, c, ALU.mult).then_inc(w.term, 1)
                    wait_gates(3)
                    V.tensor_tensor(i, i, g, ALU.mult).then_inc(w.term, 1)
                    dve.wait_ge(w.term, it * (2 * (p - 1)) + 2 * j)
                    V.tensor_tensor(c, c, i, ALU.add).then_inc(w.cell_ready, 1)

            def h_places(p, it, j, s):
                if j == p - 1 and p < 4:
                    return windows_bt(hT, p, it, s, j), windows(h_hi, p, it, s, j), windows(h_lo, p, it, s, j)
                return tuple(tb(x[:, s, :], p) for x in (hbuf, hs_hi, hs_lo))

            def step_full(p, it, j, s):
                w = win[p][s]
                dve.wait_ge(w.gate_read.sem, w.gate_read.at(it * gates_before(p), gates_before(j + 1)))
                dve.wait_ge(w.tanh_ready, it * p + (j + 1))
                V.tensor_tensor(h_places(p, it, j, s)[0], tb(go[:, s, :], p), tb(gg[:, s, :], p),
                                ALU.mult).then_inc(w.h_full, 1)

            def step_parts(p, it, j, s):
                w = win[p][s]
                full, hi, lo = h_places(p, it, j, s)
                dve.wait_ge(w.h_full, it * p + (j + 1))
                if p == 4 and j == 3:
                    dve.wait_ge(xres_in, 16)
                    x_at = windows_bt(x_res, p, it, s, j)
                    V.tensor_tensor(x_at, x_at, full, ALU.add).then_inc(w.h_ready.sem, 1)
                    return
                V.tensor_copy(hi, full).then_inc(w.h_hi, 1)
                dve.wait_ge(w.h_hi, it * min(p, 3) + (j + 1))
                V.tensor_tensor(lo, full, hi.bitcast(F32), ALU.subtract).then_inc(w.h_ready.sem, 1)

            def window_steps(steps, left=None):
                for step in steps:
                    p, it, j, s = step
                    step_cell(*step)
                    if left:
                        step_parts(*left)
                    step_full(*step)
                    left = step if j == p - 1 else None
                    if not left:
                        step_parts(*step)
                return left

            dve.wait_ge(lw_ready, 7)
            for p in WIN:
                left = window_steps(steps_of_pair(p, 0, (p - 1, PAIRS[p - 1] - 1, p - 2, 1) if p > 2 else None))
                assert left is None
                with dve.Fori(1, PAIRS[p]) as it:
                    left = window_steps(steps_of_pair(p, it, (p, it - 1, p - 1, 1)))
                    assert left is None
            step_parts(*window_steps([(4, PAIRS[4] - 1, 3, 1)]))

            LN_STEPS = 4 + 4 + 1

            def ln_scalars(st, var_sem, sd_sem, count, half=0):
                me, qe, mo, qo = (lnst[:, half, :, k] for k in (1, 2, 4, 5))
                msum, dif, ssq, t, r, v, sd, nm = (lnsm[:, half, k, :] for k in range(8))
                st.settle()
                st.then(V.tensor_tensor(dif, me, mo, ALU.subtract))
                st.then(V.scalar_tensor_tensor(out=ssq, in0=qe, scalar=EPS * P, in1=qo, op0=ALU.add, op1=ALU.add))
                st.settle()
                st.then(V.scalar_tensor_tensor(out=dif, in0=dif, scalar=0.25, in1=dif, op0=ALU.mult,
                                               op1=ALU.mult))
                st.settle()
                V.scalar_tensor_tensor(out=v, in0=ssq, scalar=1.0 / P, in1=dif, op0=ALU.mult,
                                       op1=ALU.add).then_inc(var_sem, 1)
                st.then(V.tensor_tensor(msum, me, mo, ALU.add))
                dve.wait_ge(sd_sem, count)
                newton(st, v, sd, r, t)
                st.then(V.scalar_tensor_tensor(out=nm, in0=msum, scalar=-0.5, in1=r, op0=ALU.mult,
                                               op1=ALU.mult))
                st.settle()

            def w1_stats(it, q, h):
                dve.wait_ge(w1_read.sem, w1_read.at(it * (HC * Q), HC * q + h + 1))
                V.bn_stats(st1[:, h, bass.ds(it * Q + q, 1), :].rearrange("p a s -> p (a s)"),
                           h1[:, h, grp(it * Q + q)]).then_inc(st1_done, 1)

            it_is_first = lambda it: isinstance(it, int) and it == 0

            def layer_norm(it, back):
                steps = Q * GB + LN_STEPS
                st = Steps(dve, ln_step, it * steps)
                for q in range(Q):
                    dve.wait_ge(res_t_done, it * Q + (q + 1))
                    for k in range(GB):
                        st.then(V.bn_stats(lnst[:, 0, q * GB + k, :], bank[q][:, k * P:(k + 1) * P]))
                    for h in range(HC):
                        if q == 0 and back:
                            w1_stats(it - 2, 1, h)
                        elif q == 1 and back:
                            w1_stats(it - 2, 2, h)
                if not it_is_first(it):
                    dve.wait_ge(x1_act, it * (Q - 1))
                ln_scalars(st, ln_var, ln_sd, it + 1)
                assert st.n == steps
                if not it_is_first(it):
                    dve.wait_ge(agg_done, it * Q + (1 - Q))
                    dve.wait_ge(x1_saved[0], it * 16)
                for k in range(GB):
                    last = V.tensor_scalar(x1s[:, 0, k * P:(k + 1) * P], bank[0][:, k * P:(k + 1) * P],
                                           lnsm[:, 0, 4, k:k + 1], lnsm[:, 0, 7, k:k + 1], ALU.mult, ALU.add)
                    if k == 0:
                        last.then_inc(ln_ready, 1)
                    elif k == GB - 1:
                        last.then_inc(x1_dve, 1)
                for h in range(HC if back else 0):
                    w1_stats(it - 2, 3, h)
                for h in range(0 if it_is_first(it) else HC):
                    w1_stats(it - 1, 0, h)

            layer_norm(0, False)
            layer_norm(1, False)
            with dve.Fori(2, ITERS) as it:
                layer_norm(it, True)
            for g in range((ITERS - 2) * Q + 1, ITERS * Q):
                for h in range(HC):
                    w1_stats(g // Q, g % Q, h)

            bst = Steps(dve, bn_step)

            def bn_scalars(c0, n, g0, be0, count):
                v, sd, r, t, neg = (bnsm[:, k, c0:c0 + n] for k in range(5))
                scale = bnsm[:, 6, c0:c0 + n]
                mean, var = mv[:, c0:c0 + n, 0], mv[:, c0:c0 + n, 1]
                bst.settle()
                V.tensor_scalar(v, var, EPS, None, ALU.add).then_inc(bn_var, 1)
                bst.then(V.tensor_scalar(neg, mean, -1.0, None, ALU.mult))
                dve.wait_ge(bn_sd, count)
                newton(bst, v, sd, r, t)
                bst.then(V.tensor_tensor(scale, r, vecs[:, g0:g0 + n], ALU.mult))
                bst.settle()
                for c in range(n):
                    shift, beta = bnsm[:, 7, c0 + c:c0 + c + 1], vecs[:, be0 + c:be0 + c + 1]
                    last = V.scalar_tensor_tensor(out=shift, in0=bnsm[:, 6, c0 + c:c0 + c + 1],
                                                  scalar=bnsm[:, 4, c0 + c:c0 + c + 1], in1=beta,
                                                  op0=ALU.mult, op1=ALU.add)
                last.then_inc(bn_ready, 1)

            dve.wait_ge(st1_done, HC * G)
            for h in range(HC):
                bst.then(V.bn_aggr(mv[:, h, :], st1[:, h, :, :].rearrange("p a s -> p (a s)")))
            bn_scalars(0, HC, V_G1, V_BE1, 1)

            with dve.Fori(0, ITERS) as it:
                for q in range(Q):
                    dve.wait_ge(w2_done.sem, w2_done.at(it * Q, q + 1))
                    V.tensor_scalar(outT[:, grp(it * Q + q)], bank[q][:, :], vecs[:, V_B2:V_B2 + 1], None,
                                    ALU.add).then_inc(w2_read.sem, 1)
                    dve.wait_ge(w2_read.sem, w2_read.at(it * Q, q + 1))
                    V.bn_stats(st2[:, bass.ds(it * Q + q, 1), :].rearrange("p a s -> p (a s)"),
                               outT[:, grp(it * Q + q)]).then_inc(st2_done, 1)
            dve.wait_ge(st2_done, G)
            bst.then(V.bn_aggr(mv[:, 2, :], st2[:, :, :].rearrange("p a s -> p (a s)")))
            bn_scalars(2, 1, V_G2, V_BE2, 2)

            for r in range(ITERS):
                half = r % 2
                st = Steps(dve, ln2_step, r * (Q * GB + LN_STEPS))
                for q in range(Q):
                    dve.wait_ge(sum_done, r * Q + q + 1)
                    for k in range(GB):
                        st.then(V.bn_stats(lnst[:, half, q * GB + k, :], sum_bank(r, q)[:, k * P:(k + 1) * P]))
                if r >= 2:
                    dve.wait_ge(*normalised(r - 2, act_groups(r - 2)[-1]))
                ln_scalars(st, ln2_var, ln2_sd, r + 1, half)
                for q in dve_groups(r):
                    for k in range(GB):
                        c = q * GB + k
                        last = V.tensor_scalar(x1[:, r * Q * GB + c, :], sum_bank(r, q)[:, k * P:(k + 1) * P],
                                               lnsm[:, half, 4, c:c + 1], lnsm[:, half, 7, c:c + 1],
                                               ALU.mult, ALU.add)
                        if c == dve_groups(r).start * GB:
                            last.then_inc(ln2_ready, 1)
                        elif k == GB - 1:
                            last.then_inc(out_dve, 1)


def kernel(x, adj, L0_gnn_Wg0, L0_gnn_bg0, L0_gnn_Wg1, L0_gnn_bg1, L0_gnn_Wih, L0_gnn_Whh, L0_gnn_bih,
           L0_gnn_bhh, L1_gnn_W1, L1_gnn_b1, L1_gnn_g1, L1_gnn_be1, L1_gnn_W2, L1_gnn_b2, L1_gnn_g2,
           L1_gnn_be2):
    import numpy as np
    import concourse.bacc as bacc
    from concourse.bass_utils import run_bass_kernel_spmd

    a = np.asarray
    adj = a(adj)
    row = lambda v: np.broadcast_to(a(v)[None, :], (P, P))
    w2 = a(L1_gnn_W2).T.reshape(HC, P, P).transpose(1, 0, 2).reshape(P, HC * P)
    by_gate = lambda v: a(v).reshape(16, P).T
    chan = lambda v: a(v).reshape(-1, P).T
    wT = lambda w: a(w).transpose(2, 0, 1)
    arrays = {
        "xT": np.ascontiguousarray(a(x).transpose(2, 0, 1)),
        "mats": np.ascontiguousarray(np.concatenate(
            [a(L0_gnn_Wg0), row(L0_gnn_bg0), adj.T, adj, a(L0_gnn_Wg1), row(L0_gnn_bg1),
             a(L1_gnn_W1).T, w2], axis=1)),
        "lw": np.ascontiguousarray(np.concatenate([wT(L0_gnn_Wih), wT(L0_gnn_Whh)[:, 1:]], axis=1)),
        "vecs": np.ascontiguousarray(np.concatenate(
            [by_gate(L0_gnn_bih), by_gate(L0_gnn_bhh), chan(L1_gnn_b1), chan(L1_gnn_g1), chan(L1_gnn_be1),
             chan(L1_gnn_b2), chan(L1_gnn_g2), chan(L1_gnn_be2)], axis=1)),
    }
    nc = bacc.Bacc("TRN2", target_bir_lowering=False, num_devices=1)
    ins = [nc.dram_tensor(k + "_dram", v.shape, F32, kind="ExternalInput").ap() for k, v in arrays.items()]
    out = nc.dram_tensor("out_dram", (T, B, P), F32, kind="ExternalOutput").ap()
    build(nc, *ins, out)
    r = run_bass_kernel_spmd(nc, [{k + "_dram": v for k, v in arrays.items()}], core_ids=[0])
    return np.ascontiguousarray(r.results[0]["out_dram"].transpose(1, 0, 2))
```
